# Optimizing a Trainium2 kernel written in Bass

```python
import numpy as np
import jax
import jax.numpy as jnp

def _softmax(x, axis=-1):
    return jax.nn.softmax(x, axis=axis)

def _gelu(x):
    return jax.nn.gelu(x, approximate=True)

def _silu(x):
    return jax.nn.silu(x)

def _sigmoid(x):
    return jax.nn.sigmoid(x)

def _layernorm(x, axis=-1, eps=1e-05):
    m = jnp.mean(x, axis=axis, keepdims=True)
    v = jnp.var(x, axis=axis, keepdims=True)
    return (x - m) / jnp.sqrt(v + eps)

def _scatter_add(tgt, idx, src, axis=0):
    return tgt.at[idx].add(src)

def _segment_sum(src, seg, n):
    return jax.ops.segment_sum(src, seg, n)
kernel_name = 'mk_perceiver_d1_seqx_r4_a28677'

def setup_inputs(seed: int=0):
    np.random.seed(seed)
    _w = jnp.asarray

    def _rec_inputs():
        import jax
        import jax.numpy as jnp
        _rk = jax.random.key(seed)
        x = 7.22e-05 + 1 * jax.random.normal(jax.random.fold_in(_rk, 1), (64, 64, 256), jnp.float32)
        _lenS = 64 - jax.random.randint(jax.random.fold_in(_rk, 7), (64,), 0, max(1, 64 // 4) + 1, jnp.int32)
        _lenS2 = 256 - jax.random.randint(jax.random.fold_in(_rk, 8), (64,), 0, max(1, 256 // 4) + 1, jnp.int32)
        _ctx_1024P = jax.random.normal(jax.random.fold_in(_rk, 11), (64, 16, 256), jnp.float32)
        _ctx_1024c = jax.random.dirichlet(jax.random.fold_in(_rk, 511), 0.3 * jnp.ones((16,), jnp.float32), (64, 256))
        _ctx_1024t = jnp.einsum('bsk,bkd->bsd', _ctx_1024c, _ctx_1024P)
        _ctx_1024t = _ctx_1024t * jax.lax.rsqrt(jnp.mean(jnp.square(_ctx_1024t)) + 1e-12) * 0.953939
        ctx_1024 = 4.13588e-05 + 0.999923 * (_ctx_1024t + 0.3 * jax.random.normal(jax.random.fold_in(_rk, 611), (64, 256, 256), jnp.float32))
        return (x, ctx_1024)
    x, ctx_1024 = _rec_inputs()

    def _L0_xattn_setup():
        import jax, jax.numpy as jnp
        import numpy as np
        N_HEAD, MODEL_DIM, KEY_DIM, VALUE_DIM = (16, 256, 64, 64)
        B, S = (4, 512)
        EPS = 1e-05
        TEMP = float(np.sqrt(KEY_DIM))
        key = jax.random.key(seed)
        ks = jax.random.split(key, 12)
        d = {'query': jax.random.normal(ks[0], (B, S, MODEL_DIM), jnp.float32), 'key': jax.random.normal(ks[1], (B, S, MODEL_DIM), jnp.float32), 'value': jax.random.normal(ks[2], (B, S, MODEL_DIM), jnp.float32), 'Wq': jax.random.normal(ks[3], (MODEL_DIM, N_HEAD * KEY_DIM), jnp.float32) * np.sqrt(2.0 / (MODEL_DIM + KEY_DIM)), 'bq': jnp.zeros((N_HEAD * KEY_DIM,), jnp.float32), 'Wk': jax.random.normal(ks[4], (MODEL_DIM, N_HEAD * KEY_DIM), jnp.float32) * np.sqrt(2.0 / (MODEL_DIM + KEY_DIM)), 'bk': jnp.zeros((N_HEAD * KEY_DIM,), jnp.float32), 'Wv': jax.random.normal(ks[5], (MODEL_DIM, N_HEAD * VALUE_DIM), jnp.float32) * np.sqrt(2.0 / (MODEL_DIM + VALUE_DIM)), 'bv': jnp.zeros((N_HEAD * VALUE_DIM,), jnp.float32), 'Wo': jax.random.normal(ks[6], (N_HEAD * VALUE_DIM, MODEL_DIM), jnp.float32) * np.sqrt(2.0 / (N_HEAD * VALUE_DIM + MODEL_DIM)), 'bo': jnp.zeros((MODEL_DIM,), jnp.float32), 'ln_gamma': jnp.ones((MODEL_DIM,), jnp.float32), 'ln_beta': jnp.zeros((MODEL_DIM,), jnp.float32)}
        return d
    _L0_xattn_all = _L0_xattn_setup()
    _L0_xattn_in = {k: v for k, v in _L0_xattn_all.items() if k in ('Wq', 'bq', 'Wk', 'bk', 'Wv', 'bv', 'Wo', 'bo', 'ln_gamma', 'ln_beta')}
    del _L0_xattn_all

    def _L0_attn_setup():
        import jax, jax.numpy as jnp
        import numpy as np
        D_MODEL = 256
        NUM_HEADS = 16
        HEAD_DIM = D_MODEL // NUM_HEADS
        ROPE_BASE = 100000.0

        def _rope_tables(seq_len):
            dim_pairs = HEAD_DIM // 2
            freqs = 1.0 / ROPE_BASE ** (jnp.arange(dim_pairs, dtype=jnp.float32) / dim_pairs)
            pos = jnp.arange(seq_len, dtype=jnp.float32)
            angles = jnp.outer(pos, freqs)
            return (jnp.cos(angles), jnp.sin(angles))

        def _apply_rope(x, cos, sin):
            d = x.shape[-1]
            x1, x2 = (x[..., :d // 2], x[..., d // 2:])
            x1r = x1 * cos - x2 * sin
            x2r = x1 * sin + x2 * cos
            return jnp.concatenate([x1r, x2r], axis=-1)
        key = jax.random.key(seed)
        ks = jax.random.split(key, 9)
        B, N, D = (4, 512, D_MODEL)
        s = 1.0 / np.sqrt(D)
        inp = {'x': jax.random.normal(ks[0], (B, N, D), dtype=jnp.float32), 'Wq': jax.random.uniform(ks[1], (D, D), jnp.float32, -s, s), 'bq': jax.random.uniform(ks[2], (D,), jnp.float32, -s, s), 'Wk': jax.random.uniform(ks[3], (D, D), jnp.float32, -s, s), 'bk': jax.random.uniform(ks[4], (D,), jnp.float32, -s, s), 'Wv': jax.random.uniform(ks[5], (D, D), jnp.float32, -s, s), 'bv': jax.random.uniform(ks[6], (D,), jnp.float32, -s, s), 'Wo': jax.random.uniform(ks[7], (D, D), jnp.float32, -s, s), 'bo': jax.random.uniform(ks[8], (D,), jnp.float32, -s, s)}
        return inp
    _L0_attn_all = _L0_attn_setup()
    _L0_attn_in = {k: v for k, v in _L0_attn_all.items() if k in ('Wq', 'bq', 'Wk', 'bk', 'Wv', 'bv', 'Wo', 'bo')}
    del _L0_attn_all

    def _L0_ffn_setup():
        import jax, jax.numpy as jnp
        import numpy as np
        D_MODEL, FF_DIM = (256, 512)
        N_SHARED, N_ROUTED, TOP_K = (1, 8, 2)
        BATCH, SEQ = (2, 512)
        key = jax.random.key(seed)
        ks = jax.random.split(key, 8)
        init = lambda k, shape: jax.random.normal(k, shape, jnp.float32) * 0.02
        x = jax.random.normal(ks[0], (BATCH, SEQ, D_MODEL), jnp.float32)
        Wg = init(ks[1], (D_MODEL, N_ROUTED))
        Ws1 = init(ks[2], (D_MODEL, FF_DIM))
        Ws3 = init(ks[3], (D_MODEL, FF_DIM))
        Ws2 = init(ks[4], (FF_DIM, D_MODEL))
        We1 = init(ks[5], (N_ROUTED, D_MODEL, FF_DIM))
        We3 = init(ks[6], (N_ROUTED, D_MODEL, FF_DIM))
        We2 = init(ks[7], (N_ROUTED, FF_DIM, D_MODEL))
        return {'x': x, 'Wg': Wg, 'Ws1': Ws1, 'Ws3': Ws3, 'Ws2': Ws2, 'We1': We1, 'We3': We3, 'We2': We2}
    _L0_ffn_all = _L0_ffn_setup()
    _L0_ffn_in = {k: v for k, v in _L0_ffn_all.items() if k in ('Wg', 'Ws1', 'Ws3', 'Ws2', 'We1', 'We3', 'We2')}
    del _L0_ffn_all
    return {'x': x, 'ctx_1024': ctx_1024, 'L0_xattn_Wq': _L0_xattn_in['Wq'], 'L0_xattn_bq': _L0_xattn_in['bq'], 'L0_xattn_Wk': _L0_xattn_in['Wk'], 'L0_xattn_bk': _L0_xattn_in['bk'], 'L0_xattn_Wv': _L0_xattn_in['Wv'], 'L0_xattn_bv': _L0_xattn_in['bv'], 'L0_xattn_Wo': _L0_xattn_in['Wo'], 'L0_xattn_bo': _L0_xattn_in['bo'], 'L0_xattn_ln_gamma': _L0_xattn_in['ln_gamma'], 'L0_xattn_ln_beta': _L0_xattn_in['ln_beta'], 'L0_attn_Wq': _L0_attn_in['Wq'], 'L0_attn_bq': _L0_attn_in['bq'], 'L0_attn_Wk': _L0_attn_in['Wk'], 'L0_attn_bk': _L0_attn_in['bk'], 'L0_attn_Wv': _L0_attn_in['Wv'], 'L0_attn_bv': _L0_attn_in['bv'], 'L0_attn_Wo': _L0_attn_in['Wo'], 'L0_attn_bo': _L0_attn_in['bo'], 'L0_ffn_Wg': _L0_ffn_in['Wg'], 'L0_ffn_Ws1': _L0_ffn_in['Ws1'], 'L0_ffn_Ws3': _L0_ffn_in['Ws3'], 'L0_ffn_Ws2': _L0_ffn_in['Ws2'], 'L0_ffn_We1': _L0_ffn_in['We1'], 'L0_ffn_We3': _L0_ffn_in['We3'], 'L0_ffn_We2': _L0_ffn_in['We2']}

def reference(x, ctx_1024, L0_xattn_Wq, L0_xattn_bq, L0_xattn_Wk, L0_xattn_bk, L0_xattn_Wv, L0_xattn_bv, L0_xattn_Wo, L0_xattn_bo, L0_xattn_ln_gamma, L0_xattn_ln_beta, L0_attn_Wq, L0_attn_bq, L0_attn_Wk, L0_attn_bk, L0_attn_Wv, L0_attn_bv, L0_attn_Wo, L0_attn_bo, L0_ffn_Wg, L0_ffn_Ws1, L0_ffn_Ws3, L0_ffn_Ws2, L0_ffn_We1, L0_ffn_We3, L0_ffn_We2):
    import jax
    import jax.numpy as jnp

    def _L0_xattn_ref(query, key, value, Wq, bq, Wk, bk, Wv, bv, Wo, bo, ln_gamma, ln_beta):
        import jax, jax.numpy as jnp
        import numpy as np
        N_HEAD, MODEL_DIM, KEY_DIM, VALUE_DIM = (16, 256, 64, 64)
        B, S = (4, 512)
        EPS = 1e-05
        TEMP = float(np.sqrt(KEY_DIM))
        b, sq, _ = query.shape
        residual = query
        q = (query @ Wq + bq).reshape(b, sq, N_HEAD, KEY_DIM)
        k = (key @ Wk + bk).reshape(b, key.shape[1], N_HEAD, KEY_DIM)
        v = (value @ Wv + bv).reshape(b, value.shape[1], N_HEAD, VALUE_DIM)
        scores = jnp.einsum('bqhd,bkhd->bhqk', q, k) / TEMP
        attn = jax.nn.softmax(scores, axis=-1)
        out = jnp.einsum('bhqk,bkhd->bqhd', attn, v).reshape(b, sq, N_HEAD * VALUE_DIM)
        out = out @ Wo + bo + residual
        mu = jnp.mean(out, axis=-1, keepdims=True)
        var = jnp.var(out, axis=-1, keepdims=True)
        return (out - mu) * jax.lax.rsqrt(var + EPS) * ln_gamma + ln_beta

    def _L0_attn_ref(x, Wq, bq, Wk, bk, Wv, bv, Wo, bo):
        import jax, jax.numpy as jnp
        import numpy as np
        D_MODEL = 256
        NUM_HEADS = 16
        HEAD_DIM = D_MODEL // NUM_HEADS
        ROPE_BASE = 100000.0

        def _rope_tables(seq_len):
            dim_pairs = HEAD_DIM // 2
            freqs = 1.0 / ROPE_BASE ** (jnp.arange(dim_pairs, dtype=jnp.float32) / dim_pairs)
            pos = jnp.arange(seq_len, dtype=jnp.float32)
            angles = jnp.outer(pos, freqs)
            return (jnp.cos(angles), jnp.sin(angles))

        def _apply_rope(x, cos, sin):
            d = x.shape[-1]
            x1, x2 = (x[..., :d // 2], x[..., d // 2:])
            x1r = x1 * cos - x2 * sin
            x2r = x1 * sin + x2 * cos
            return jnp.concatenate([x1r, x2r], axis=-1)
        B, N, D = x.shape
        H, Hd = (NUM_HEADS, HEAD_DIM)
        scale = Hd ** (-0.5)
        q = (x @ Wq.T + bq).reshape(B, N, H, Hd).transpose(0, 2, 1, 3)
        k = (x @ Wk.T + bk).reshape(B, N, H, Hd).transpose(0, 2, 1, 3)
        v = (x @ Wv.T + bv).reshape(B, N, H, Hd).transpose(0, 2, 1, 3)
        cos, sin = _rope_tables(N)
        q = _apply_rope(q, cos, sin)
        k = _apply_rope(k, cos, sin)
        scores = jnp.einsum('bhqd,bhkd->bhqk', q, k) * scale
        attn = jax.nn.softmax(scores, axis=-1)
        out = jnp.einsum('bhqk,bhkd->bhqd', attn, v)
        out = out.transpose(0, 2, 1, 3).reshape(B, N, D)
        return out @ Wo.T + bo

    def _L0_ffn_ref(x, Wg, Ws1, Ws3, Ws2, We1, We3, We2):
        import jax, jax.numpy as jnp
        import numpy as np
        D_MODEL, FF_DIM = (256, 512)
        N_SHARED, N_ROUTED, TOP_K = (1, 8, 2)
        BATCH, SEQ = (2, 512)
        B, S, d = x.shape
        E = Wg.shape[1]
        xf = x.reshape(-1, d)
        T = xf.shape[0]
        gates = jax.nn.sigmoid(xf @ Wg)
        vals, idx = jax.lax.top_k(gates, TOP_K)
        vals = vals / vals.sum(axis=-1, keepdims=True)
        w = jnp.zeros((T, E), x.dtype).at[jnp.arange(T)[:, None], idx].add(vals)
        shared = jax.nn.silu(xf @ Ws1) * (xf @ Ws3) @ Ws2
        h = jax.nn.silu(jnp.einsum('td,edf->tef', xf, We1)) * jnp.einsum('td,edf->tef', xf, We3)
        routed = jnp.einsum('tef,efd,te->td', h, We2, w)
        out = (shared + routed) / (N_SHARED + TOP_K)
        return out.reshape(B, S, d)
    x = x + _L0_xattn_ref(_layernorm(x, axis=-1), ctx_1024, ctx_1024, L0_xattn_Wq, L0_xattn_bq, L0_xattn_Wk, L0_xattn_bk, L0_xattn_Wv, L0_xattn_bv, L0_xattn_Wo, L0_xattn_bo, L0_xattn_ln_gamma, L0_xattn_ln_beta)
    x = x + _L0_attn_ref(_layernorm(x, axis=-1), L0_attn_Wq, L0_attn_bq, L0_attn_Wk, L0_attn_bk, L0_attn_Wv, L0_attn_bv, L0_attn_Wo, L0_attn_bo)
    x = x + _L0_ffn_ref(_layernorm(x, axis=-1), L0_ffn_Wg, L0_ffn_Ws1, L0_ffn_Ws3, L0_ffn_Ws2, L0_ffn_We1, L0_ffn_We3, L0_ffn_We2)
    return x

_drawn_inputs = setup_inputs


def setup_inputs(seed=0):
    import zlib

    import numpy as np

    out = dict(_drawn_inputs(seed))
    spreads = {'L0_xattn_bq': (0.0, 0.345),
     'L0_xattn_bk': (0.0, 0.8),
     'L0_xattn_bv': (0.0, 0.1),
     'L0_xattn_bo': (0.0, 0.1),
     'L0_xattn_ln_gamma': (1.0, 0.2),
     'L0_xattn_ln_beta': (0.0, 0.1)}
    factors = {'L0_attn_Wq': 7.522,
     'L0_attn_bq': 8.0,
     'L0_attn_Wk': 7.329,
     'L0_attn_bk': 8.0,
     'L0_attn_bv': 5.294,
     'L0_attn_bo': 3.035,
     'L0_ffn_Wg': 8.0,
     'L0_ffn_Ws1': 8.0,
     'L0_ffn_Ws3': 8.0,
     'L0_ffn_Ws2': 8.0,
     'L0_ffn_We1': 8.0,
     'L0_ffn_We3': 8.0,
     'L0_ffn_We2': 8.0}
    for name, (base, spread) in spreads.items():
        noise = np.random.default_rng([zlib.crc32(name.encode()), seed]).standard_normal(out[name].shape)
        drawn = base * np.exp(spread * noise) if base else spread * noise
        out[name] = jnp.asarray(drawn.astype(out[name].dtype))
    for name, factor in factors.items():
        out[name] = (out[name] * factor).astype(out[name].dtype)
    return out
```

```python
from contextlib import ExitStack

import numpy as np
import concourse.bass as bass
from concourse import mybir

F32 = mybir.dt.float32
F32R = mybir.dt.float32r
I32 = mybir.dt.int32
U32 = mybir.dt.uint32
ALU = mybir.AluOpType
ACT = mybir.ActivationFunctionType
AX_X = mybir.AxisListType.X
P = 128
D = 256
DC = D // P
BATCH = 64
SQ = 64
SK = 256
KC = SK // P
HEADS = 16
DK = 64
EPS = 1e-5
GB = 4
GROUPS = BATCH // GB
GT = GB * SQ
TILES = GT // P
HALF = HEADS // 2
PAIRS = HALF // 2
STEPS = 2 * GB
SCALE = 1.0 / float(np.sqrt(DK))
RING = 4
LINKS_PER_GROUP = 47


class Turns:

    def __init__(self, order, first, last, peeled=2):
        ends = range(last - peeled + 1, last + 1)
        self.order = {g: order(g) for g in (*range(first, 2), *ends)}
        self.before, n = {}, 0
        self.loop = len(self.order[1])
        for g in range(first, 2):
            self.before[g] = n
            n += len(self.order[g])
        n = self.before[1] + (ends[0] - 1) * self.loop
        for g in ends:
            self.before[g] = n
            n += len(self.order[g])

    def index(self, g, key):
        if isinstance(g, int):
            k = g if g in self.order else 1
            return self.before[k] + (g - k) * self.loop + self.order[k].index(key), 0
        return self.before[1] - self.loop + self.order[1].index(key), self.loop


class Group:

    def __init__(self, at, kind):
        self.at, self.kind = at, kind
        self.cur = kind in (0, 1, GROUPS - 1)
        self.next = kind in (-1, 0, 1)
        self.prev = kind in (1, GROUPS - 1, GROUPS)


def turns(eng):
    yield Group(-1, -1)
    yield Group(0, 0)
    with eng.Fori(1, GROUPS - 1) as g:
        yield Group(g, 1)
    yield Group(GROUPS - 1, GROUPS - 1)
    yield Group(GROUPS, GROUPS)


def ring_order(kind):
    g = Group(None, kind)
    out = []
    if kind == -1:
        out += [("ctxT", b) for b in range(GB)]
        out.append(("xT",))
        out += [("q", 1, m) for m in range(2)]
        out += [("fold", 1, h) for h in range(HALF)]
        out.append(("qbk",))
        return out
    for s in range(STEPS):
        half, b = divmod(s, GB)
        if half == 1 and g.next:
            out.append(("ctxT", b))
        if b == 2 and (g.cur if half else g.prev):
            out += [("v", half, j) for j in range(2)]
        if s == 3 and g.prev:
            out += [("o", t) for t in range(TILES)]
        if s == 6 and g.next:
            out.append(("xT",))
        if (g.cur if s >= 2 else g.prev):
            out += [("pc", s, c) for c in range(DC)]
        if b == 3 and (g.next if half else g.cur):
            out += [("fold", half, h) for h in range(HALF)]
        if s == 7 and g.next:
            out.append(("qbk",))
        if (g.cur if s >= 1 else g.prev):
            out += [("pt", s, k) for k in range(KC)]
        if b == 2 and (g.next if half else g.cur):
            out += [("q", half, m) for m in range(2)]
    return out


def cross_attention(nc, t, x1_dram):
    with ExitStack() as ctx:
        def sb(name, shape, dt=F32):
            return ctx.enter_context(nc.sbuf_tensor(name, shape, dt))

        def sem(name):
            return ctx.enter_context(nc.semaphore(name))

        ident = sb("ident", [P, P])
        wq_hi = sb("wq_hi", [P, DC, HEADS * DK], F32R)
        wq_lo = sb("wq_lo", [P, DC, HEADS * DK], F32R)
        wk_hi = sb("wk_hi", [P, HEADS, D], F32R)
        wk_lo = sb("wk_lo", [P, HEADS, D], F32R)
        wv = sb("wv", [P, DC, HEADS * DK])
        wo = sb("wo", [P, HALF, D])
        bq = sb("bq", [P, HALF])
        bq_low = sb("bq_low", [DK, HEADS])
        bv = sb("bv", [P, HALF])
        wqb = sb("wqb", [P, DC + 1, HEADS])
        wqb_hi = sb("wqb_hi", [P, DC, HEADS], F32R)
        wqb_lo = sb("wqb_lo", [P, DC, HEADS], F32R)
        qbk = sb("qbk", [P, GB, HALF])
        bo = sb("bo", [P, D])
        gamma = sb("gamma", [P, D])
        beta = sb("beta", [P, D])
        power = sb("power", [P, TILES])
        ctx_raw = sb("ctx_raw", [P, GB, KC, D])
        ctx_hi = sb("ctx_hi", [P, GB, KC, D], F32R)
        ctx_lo = sb("ctx_lo", [P, GB, KC, D], F32R)
        ctxT_hi = sb("ctxT_hi", [P, GB, DC, SK], F32R)
        ctxT_lo = sb("ctxT_lo", [P, GB, DC, SK], F32R)
        x_in = sb("x_in", [P, TILES, D])
        x_again = sb("x_again", [P, TILES, D])
        xln = sb("xln", [P, TILES, D])
        resid = sb("resid", [P, TILES, D])
        z = sb("z", [P, TILES, D])
        stats = sb("stats", [P, 2, TILES, 6])
        mv = sb("mv", [P, 2, TILES, 2])
        rstd = sb("rstd", [P, 2, TILES])
        xT_hi = sb("xT_hi", [P, DC, GT], F32R)
        xT_lo = sb("xT_lo", [P, DC, GT], F32R)
        q_st = sb("q_st", [P, HALF, GT], F32R)
        qk_hi = sb("qk_hi", [P, DC, GB, HALF, SQ], F32R)
        qk_lo = sb("qk_lo", [P, DC, GB, HALF, SQ], F32R)
        probs = sb("probs", [P, 2, PAIRS, SK])
        peak = sb("peak", [P, 2, PAIRS])
        top = sb("top", [P, 2, PAIRS])
        nbias = sb("nbias", [P, 2, PAIRS])
        rsum = sb("rsum", [P, 2, PAIRS])
        rinv = sb("rinv", [P, 2, PAIRS])
        pT_hi = sb("pT_hi", [P, KC, HALF * SQ], F32R)
        pT_lo = sb("pT_lo", [P, KC, HALF * SQ], F32R)
        pc = sb("pc", [P, DC, HALF, GT])
        oT = sb("oT", [P, HALF, GT])
        wstage = pc[:, :, :, :].rearrange("p c h n -> p (c h n)")
        biases = oT[:, :, :].rearrange("p h n -> p (h n)").rearrange("p (i n) -> p i n", i=2)
        products = probs[:, :, :, :].rearrange("p s i k -> p s (i k)")

        scores = ctx.enter_context(nc.psum_tensor("scores", [P, 2, 2, 512], F32))
        ring = ctx.enter_context(nc.psum_tensor("ring", [P, RING, 512], F32))

        weights_in = sem("weights_in")
        small_in = sem("small_in")
        biases_in = sem("biases_in")
        wqb_done = sem("wqb_done")
        pool_setup = sem("pool_setup")
        setup_hi = sem("setup_hi")
        setup_lo = sem("setup_lo")
        setup_T = sem("setup_T")
        ctx_in = [sem(f"ctx_in{b}") for b in range(GB)]
        x_loaded = sem("x_loaded")
        x_reloaded = sem("x_reloaded")
        filled = [sem(f"filled{k}") for k in range(RING)]
        freed = [sem(f"freed{k}") for k in range(RING)]
        hi_done = sem("hi_done")
        scores_done = sem("scores_done")
        peak_done = sem("peak_done")
        exp_done = sem("exp_done")
        probs_done = sem("probs_done")
        ctx_split = sem("ctx_split")
        ln_stats = sem("ln_stats")
        ln_rstd = sem("ln_rstd")
        ln_done = sem("ln_done")
        resid_done = sem("resid_done")
        tail_stats = sem("tail_stats")
        tail_rstd = sem("tail_rstd")
        tail_done = sem("tail_done")
        x1_stored = sem("x1_stored")
        dve_step = sem("dve_step")
        wqb_step = sem("wqb_step")
        pool_step = sem("pool_step")
        sp_past = sem("sp_past")
        dve_past = sem("dve_past")
        pool_past = sem("pool_past")

        ring_turns = Turns(ring_order, -1, GROUPS)
        SPLIT = ("ctxT", "xT", "fold", "pt")
        hi_turns = Turns(lambda k: [i for i in ring_order(k) if i[0] in SPLIT or i[0] == "q"], -1, GROUPS)

        def place(g, key, groups_on=0):
            if isinstance(g.at, int):
                c, f = ring_turns.index(g.at + groups_on, key)
            else:
                c, f = ring_turns.index(g.at, key)
                c += ring_turns.loop * groups_on
            return c % RING, (c // RING + 1, f // RING)

        def nth_hi(g, key):
            c, f = hi_turns.index(g.at, key)
            return c + 1 + f * g.at if f else c + 1

        seen = {}

        def reach(eng, g, semaphores, k, count):
            c, f = count
            at = (id(eng), semaphores is filled, k)
            if seen.get(at, (None, 0))[0] is g and seen[at][1] >= c:
                return
            seen[at] = (g, c)
            eng.wait_ge(semaphores[k], c + f * g.at if f else c)

        def wait_filled(eng, g, key, groups_on=0):
            k, count = place(g, key, groups_on)
            reach(eng, g, filled, k, count)
            return ring[:, k, :], freed[k]

        def wait_freed(eng, g, key, groups_on=0):
            k, count = place(g, key, groups_on)
            reach(eng, g, freed, k, count)

        def bank_for(eng, g, key):
            k, (c, f) = place(g, key)
            if f or c > 1:
                reach(eng, g, freed, k, (c - 1, f))
            return ring[:, k, :], filled[k]

        assert ring_turns.loop % RING == 0 and ring_turns.loop == 64, ring_turns.loop

        x_tiles = t["x"].rearrange("b s d -> (b s) d").rearrange("(g n p) d -> g p n d", n=TILES, p=P)
        x1_tiles = x1_dram.rearrange("(g n p) d -> g p n d", n=TILES, p=P)
        ctx_tiles = t["ctx_1024"].rearrange("b (k p) d -> b p k d", p=P)

        with nc.Block() as block:
            @block.sync
            def _(sp):
                def load_ctx(g, b):
                    gn = g.at + 1
                    sp.dma_start(ctx_raw[:, b], ctx_tiles[gn * GB + b]
                                 if isinstance(gn, int) else
                                 ctx_tiles[bass.ds(gn * GB + b, 1)].rearrange("a p k d -> p (a k) d")
                                 ).then_inc(ctx_in[b], 16)

                def x_ap(tiles, gn):
                    return tiles[gn] if isinstance(gn, int) else tiles[bass.ds(gn, 1)].rearrange("a p n d -> p (a n) d")

                sp.dma_start(wstage[:, 0:2048].rearrange("p (c n) -> p c n", c=DC),
                             t["L0_xattn_Wk"].rearrange("(c p) n -> p c n", p=P)).then_inc(weights_in, 16)
                sp.dma_start(wstage[:, 2048:4096].rearrange("p (c n) -> p c n", c=DC),
                             t["L0_xattn_Wq"].rearrange("(c p) n -> p c n", p=P)).then_inc(weights_in, 16)
                sp.dma_start(bq_low[:, :], t["L0_xattn_bq"].rearrange("(h d) -> d h", d=DK),
                             allow_slow_non_contiguous=True).then_inc(small_in, 16)
                sp.dma_start(bq[:, :], t["L0_xattn_bq"].rearrange("(m p) -> p m", p=P),
                             allow_slow_non_contiguous=True).then_inc(small_in, 16)
                sp.dma_start(bv[:, :], t["L0_xattn_bv"].rearrange("(m p) -> p m", p=P),
                             allow_slow_non_contiguous=True).then_inc(small_in, 16)
                for tile, name in ((bo, "bo"), (gamma, "ln_gamma"), (beta, "ln_beta")):
                    sp.dma_start(tile[:, :], t[f"L0_xattn_{name}"].partition_broadcast(P)).then_inc(small_in, 16)
                sp.sem_inc(x1_stored, 16)
                for i, name in enumerate(("bk", "bq")):
                    sp.dma_start(biases[:, i], t[f"L0_xattn_{name}"].partition_broadcast(P)).then_inc(biases_in, 16)
                for g in turns(sp):
                    if g.kind == -1:
                        sp.dma_start(x_in[:, :, :], x_ap(x_tiles, 0)).then_inc(x_loaded, 16)
                        for b in range(GB):
                            load_ctx(g, b)
                        sp.dma_start(wv[:, :, :], t["L0_xattn_Wv"].rearrange("(c p) n -> p c n", p=P)).then_inc(small_in, 16)
                        sp.dma_start(wo[:, :, :], t["L0_xattn_Wo"].rearrange("(m p) n -> p m n", p=P)).then_inc(small_in, 16)
                        continue
                    if g.next:
                        sp.wait_ge(ln_done, g.at + 1)
                        sp.dma_start(x_in[:, :, :], x_ap(x_tiles, g.at + 1)).then_inc(x_loaded, 16)
                        for b in range(GB):
                            sp.wait_ge(ctx_split, GB * g.at + b + 1)
                            sp.sem_inc(sp_past, 1)
                            wait_filled(sp, g, ("ctxT", b), -1)
                            load_ctx(g, b)
                    if g.prev:
                        sp.dma_start(x_again[:, :, :], x_ap(x_tiles, g.at - 1)).then_inc(x_reloaded, 16)
                        sp.wait_ge(tail_done, g.at)
                        sp.dma_start(x_ap(x1_tiles, g.at - 1), z[:, :, :]).then_inc(x1_stored, 16)
                sp.wait_ge(x1_stored, 16 * (GROUPS + 1))

            @block.gpsimd
            def _(pool):
                nc.gpsimd.memset(ident[:, :], 0.0).then_inc(pool_step, 1)
                nc.gpsimd.memset(power[:, :], -0.5).then_inc(pool_setup, 1)
                pool.wait_ge(pool_step, 1)
                nc.gpsimd.affine_select(out=ident[:, :], in_=ident[:, :], compare_op=ALU.not_equal, fill=1.0,
                                        base=0, pattern=[[-1, P]], channel_multiplier=1).then_inc(pool_setup, 1)
                pool.wait_ge(pool_setup, 2)

                def split_ctx(g, b):
                    pool.wait_ge(ctx_in[b], 16 * (g.at + 2))
                    if g.cur:
                        pool_wait_pc(g, b)
                    pool.sem_inc(pool_past, 1)
                    nc.gpsimd.tensor_copy(ctx_hi[:, b], ctx_raw[:, b]).then_inc(pool_step, 1)
                    pool.wait_ge(pool_step, nstep(g, b))
                    nc.gpsimd.tensor_tensor(ctx_lo[:, b], ctx_raw[:, b], ctx_hi[:, b],
                                            ALU.subtract).then_inc(ctx_split, 1)

                def nstep(g, b):
                    return 1 + GB * (g.at + 1) + b + 1

                def pool_wait_pc(g, b):
                    s = GB + b + 2
                    if s < STEPS:
                        wait_filled(pool, g, ("pc", s, DC - 1))

                def rsqrt(g, which, ready, done, nth):
                    pool.wait_ge(ready, nth)
                    nc.gpsimd.tensor_tensor(rstd[:, which, :], mv[:, which, :, 1], power[:, :],
                                            ALU.pow).then_inc(done, 1)

                for g in turns(pool):
                    if g.kind == -1:
                        rsqrt(g, 0, ln_stats, ln_rstd, 1)
                        for b in range(GB):
                            split_ctx(g, b)
                        continue
                    if g.prev:
                        rsqrt(g, 1, tail_stats, tail_rstd, g.at)
                    if g.next:
                        rsqrt(g, 0, ln_stats, ln_rstd, g.at + 2)
                        for b in range(2):
                            split_ctx(g, b)
                        for b in range(2, GB):
                            pool.wait_ge(ctx_in[b], 16 * (g.at + 2))
                            wait_filled(pool, g, ("pc", b - 2, DC - 1), 1)
                            pool.sem_inc(pool_past, 1)
                            nc.gpsimd.tensor_copy(ctx_hi[:, b], ctx_raw[:, b]).then_inc(pool_step, 1)
                            pool.wait_ge(pool_step, nstep(g, b))
                            nc.gpsimd.tensor_tensor(ctx_lo[:, b], ctx_raw[:, b], ctx_hi[:, b],
                                                    ALU.subtract).then_inc(ctx_split, 1)

            @block.scalar
            def _(act):
                act.wait_ge(weights_in, 32)
                nc.scalar.activation(wq_hi[:, :, :], wstage[:, 2048:4096].rearrange("p (c n) -> p c n", c=DC),
                                     ACT.Identity).then_inc(setup_hi, 1)
                for j in range(4):
                    act.wait_ge(setup_T, j + 1)
                    for hp in range(2):
                        src = ring[DK * hp:DK * hp + DK, j, :].rearrange("p (m n) -> p m n", m=2)
                        for low in range(2):
                            nc.scalar.activation(wk_hi[DK * low:DK * low + DK, 4 * j + hp:4 * j + hp + 3:2, :],
                                                 src, ACT.Identity).then_inc(setup_hi, 1)

                def upper(g, key, out, bank):
                    nc.scalar.activation(out, bank, ACT.Identity).then_inc(hi_done, 1)

                def ctx_upper(g, b):
                    bank, _ = wait_filled(act, g, ("ctxT", b))
                    upper(g, None, ctxT_hi[:, b], bank.rearrange("p (c n) -> p c n", c=DC))

                def xT_upper(g):
                    bank, _ = wait_filled(act, g, ("xT",))
                    upper(g, None, xT_hi[:, :, :], bank.rearrange("p (c n) -> p c n", c=DC))

                def q_upper(g, half, m):
                    bank, _ = wait_filled(act, g, ("q", half, m))
                    target = 1 - half
                    for i in range(2):
                        for hp in range(2):
                            pair = target * PAIRS + 2 * m + i
                            last = nc.scalar.activation(
                                q_st[0:DK, 4 * m + 2 * i + hp, :], bank[DK * hp:DK * hp + DK, i * GT:(i + 1) * GT],
                                ACT.Identity, bias=bq[DK * hp:DK * hp + DK, pair:pair + 1])
                    last.then_inc(hi_done, 1)

                def fold_upper(g, half, h):
                    bank, _ = wait_filled(act, g, ("fold", half, h))
                    upper(g, None, qk_hi[:, :, :, h, :], bank.rearrange("p (c b q) -> p c b q", c=DC, b=GB))

                def pT_upper(g, s, k):
                    bank, _ = wait_filled(act, g, ("pt", s, k))
                    upper(g, None, pT_hi[:, k, :], bank)

                def exps(g, s):
                    act.wait_ge(peak_done, STEPS * g.at + s + 1)
                    for p in range(PAIRS):
                        nc.scalar.activation(probs[:, s % 2, p, :], scores[:, s % 2, p // 2, (p % 2) * SK:(p % 2 + 1) * SK],
                                             ACT.Exp, bias=nbias[:, s % 2, p:p + 1], scale=SCALE,
                                             accum_out=rsum[:, s % 2, p:p + 1]).then_inc(exp_done, 1)

                def copy_out(g, key, out, rows):
                    bank, free = wait_filled(act, g, key)
                    nc.scalar.activation(out, rows(bank), ACT.Identity).then_inc(free, 1)

                for g in turns(act):
                    if g.kind == -1:
                        for b in range(GB):
                            ctx_upper(g, b)
                        xT_upper(g)
                        for m in range(2):
                            q_upper(g, 1, m)
                        for h in range(HALF):
                            fold_upper(g, 1, h)
                        continue
                    for s in range(STEPS):
                        half, b = divmod(s, GB)
                        if half == 1 and g.next:
                            ctx_upper(g, b)
                        if b == 2 and (g.cur if half else g.prev):
                            bank, free = wait_filled(act, g, ("v", half, 0))
                            for i in range(2):
                                pair = (1 - half) * PAIRS + i
                                last = nc.scalar.activation(oT[:, pair, :], bank[:, i * GT:(i + 1) * GT], ACT.Identity,
                                                            bias=bv[:, pair:pair + 1])
                            last.then_inc(free, 1)
                        if g.cur:
                            exps(g, s)
                        if s == 6 and g.next:
                            xT_upper(g)
                        if (g.cur if s >= 2 else g.prev):
                            at = slice((s + 2) % GB * SQ, ((s + 2) % GB + 1) * SQ)
                            for c in range(DC):
                                copy_out(g, ("pc", s, c), pc[:, c, :, at], lambda x: x.rearrange("p (h q) -> p h q", h=HALF))
                        if b == 3 and (g.next if half else g.cur):
                            for h in range(HALF):
                                fold_upper(g, half, h)
                        if (g.cur if s >= 1 else g.prev):
                            for k in range(KC):
                                pT_upper(g, s, k)
                        if b == 2 and (g.next if half else g.cur):
                            for m in range(2):
                                q_upper(g, half, m)

            @block.vector
            def _(dve):
                chain = [None, 0]
                per = {}

                def link(ins):
                    chain[1] += 1
                    ins.then_inc(dve_step, 1)
                    dve.wait_ge(dve_step, chain[0] + chain[1])

                dve.wait_ge(weights_in, 32)
                dve.wait_ge(setup_hi, 1)
                nc.vector.tensor_tensor(wq_lo[:, :, :], wstage[:, 2048:4096].rearrange("p (c n) -> p c n", c=DC),
                                        wq_hi[:, :, :], ALU.subtract).then_inc(setup_lo, 1)
                for j in range(4):
                    dve.wait_ge(setup_hi, 1 + 4 * (j + 1))
                    for hp in range(2):
                        src = ring[DK * hp:DK * hp + DK, j, :].rearrange("p (m n) -> p m n", m=2)
                        for low in range(2):
                            rows = slice(DK * low, DK * low + DK)
                            heads = slice(4 * j + hp, 4 * j + hp + 3, 2)
                            nc.vector.tensor_tensor(wk_lo[rows, heads, :], src, wk_hi[rows, heads, :],
                                                    ALU.subtract).then_inc(setup_lo, 1)
                dve.wait_ge(biases_in, 32)
                sources = [wstage[:, 2048 + c * HEADS * DK:2048 + (c + 1) * HEADS * DK] for c in range(DC)] + [biases[:, 1]]
                for c, src in enumerate(sources):
                    nc.vector.tensor_tensor(products[:, 0], src, biases[:, 0], ALU.mult).then_inc(wqb_step, 1)
                    dve.wait_ge(wqb_step, 2 * c + 1)
                    nc.vector.tensor_reduce(wqb[:, c, :], products[:, 0].rearrange("p (h d) -> p h d", d=DK), AX_X,
                                            ALU.add).then_inc(wqb_step, 1)
                    dve.wait_ge(wqb_step, 2 * c + 2)
                nc.vector.tensor_copy(wqb_hi[:, :, :], wqb[:, 0:DC, :]).then_inc(wqb_step, 1)
                nc.vector.tensor_scalar(wqb[:, DC, :], wqb[:, DC, :], SCALE, None, ALU.mult).then_inc(wqb_step, 1)
                dve.wait_ge(wqb_step, 2 * DC + 4)
                nc.vector.tensor_tensor(wqb_lo[:, :, :], wqb[:, 0:DC, :], wqb_hi[:, :, :], ALU.subtract).then_inc(wqb_done, 1)
                dve.wait_ge(small_in, 16 * 8)

                def lower(g, key, out, hi, rows):
                    k, _ = place(g, key)
                    dve.wait_ge(hi_done, nth_hi(g, key))
                    nc.vector.tensor_tensor(out, rows(ring[:, k, :]), hi, ALU.subtract).then_inc(freed[k], 1)

                def ctx_lower(g, b):
                    lower(g, ("ctxT", b), ctxT_lo[:, b], ctxT_hi[:, b], lambda x: x.rearrange("p (c n) -> p c n", c=DC))

                def xT_lower(g):
                    lower(g, ("xT",), xT_lo[:, :, :], xT_hi[:, :, :], lambda x: x.rearrange("p (c n) -> p c n", c=DC))

                def q_lower(g, half, m):
                    k, _ = place(g, ("q", half, m))
                    dve.wait_ge(hi_done, nth_hi(g, ("q", half, m)))
                    target = 1 - half
                    for i in range(2):
                        for hp in range(2):
                            h = 4 * m + 2 * i + hp
                            last = nc.vector.scalar_tensor_tensor(
                                out=q_st[DK:P, h, :], in0=ring[DK * hp:DK * hp + DK, k, i * GT:(i + 1) * GT],
                                scalar=bq_low[:, target * HALF + h:target * HALF + h + 1], in1=q_st[0:DK, h, :],
                                op0=ALU.add, op1=ALU.subtract)
                    last.then_inc(freed[k], 1)

                def fold_lower(g, half, h):
                    lower(g, ("fold", half, h), qk_lo[:, :, :, h, :], qk_hi[:, :, :, h, :],
                          lambda x: x.rearrange("p (c b q) -> p c b q", c=DC, b=GB))

                def pT_lower(g, s, k):
                    lower(g, ("pt", s, k), pT_lo[:, k, :], pT_hi[:, k, :], lambda x: x)

                def peaks(g, s):
                    for j in range(2):
                        dve.wait_ge(scores_done, 2 * (STEPS * g.at + s) + j + 1)
                        last = nc.vector.tensor_reduce(peak[:, s % 2, 2 * j:2 * j + 2],
                                                scores[:, s % 2, j, :].rearrange("p (i k) -> p i k", i=2), AX_X, ALU.max)
                        if j == 0:
                            last.then_inc(dve_step, 1)
                            chain[1] += 1
                    link(last)
                    constant = qbk[:, s % GB, s // GB * PAIRS:(s // GB + 1) * PAIRS]
                    link(nc.vector.scalar_tensor_tensor(out=top[:, s % 2, :], in0=peak[:, s % 2, :], scalar=SCALE,
                                                        in1=constant, op0=ALU.mult, op1=ALU.add))
                    nc.vector.tensor_tensor(nbias[:, s % 2, :], constant, top[:, s % 2, :],
                                            ALU.subtract).then_inc(peak_done, 1)

                def keep_qbk(g):
                    bank, free = wait_filled(dve, g, ("qbk",))
                    for i in range(2):
                        rows = slice(i * SQ, (i + 1) * SQ)
                        for hp in range(2):
                            last = nc.vector.scalar_tensor_tensor(
                                out=qbk[hp * SQ:(hp + 1) * SQ, i:GB:2, :],
                                in0=bank[rows, 0:TILES * HEADS].rearrange("p (n m e) -> p n m e", n=TILES, e=2)[:, :, :, hp],
                                scalar=SCALE,
                                in1=wqb[rows, DC, :].rearrange("p (m e) -> p m e", e=2)[:, :, hp].unsqueeze(1)
                                .broadcast_to([SQ, TILES, HALF]),
                                op0=ALU.mult, op1=ALU.add)
                    last.then_inc(free, 1)

                def normalise(g, s):
                    dve.wait_ge(exp_done, PAIRS * (STEPS * g.at + s + 1))
                    link(nc.vector.reciprocal(rinv[:, s % 2, :], rsum[:, s % 2, :]))
                    for p in range(PAIRS):
                        last = nc.vector.tensor_scalar(probs[:, s % 2, p, :], probs[:, s % 2, p, :],
                                                       rinv[:, s % 2, p:p + 1], None, ALU.mult)
                    last.then_inc(probs_done, 1)

                def ln_stats_of(src, which, ready):
                    for n in range(TILES):
                        last = nc.vector.bn_stats(stats[:, which, n, :], src[:, n, :])
                        if n + 1 < TILES:
                            last.then_inc(dve_step, 1)
                            chain[1] += 1
                    link(last)
                    dve.sem_inc(dve_past, 1)
                    for n in range(TILES):
                        last = nc.vector.bn_aggr(mv[:, which, n, :], stats[:, which, n, :])
                        if n + 1 < TILES:
                            last.then_inc(dve_step, 1)
                            chain[1] += 1
                    link(last)
                    nc.vector.tensor_scalar(mv[:, which, :, 1], mv[:, which, :, 1], EPS, None,
                                            ALU.add).then_inc(ready, 1)

                def ln_apply(src, out, which):
                    for n in range(TILES):
                        last = nc.vector.tensor_scalar(out[:, n, :], src[:, n, :], mv[:, which, n, 0:1],
                                                       rstd[:, which, n:n + 1], ALU.subtract, ALU.mult)
                        if n + 1 < TILES:
                            last.then_inc(dve_step, 1)
                            chain[1] += 1
                    return last

                def both(fn, linked=False):
                    for n in range(TILES):
                        last = fn(n)
                        if n + 1 < TILES:
                            last.then_inc(dve_step, 1)
                            chain[1] += 1
                    if linked:
                        link(last)
                    return last

                for g in turns(dve):
                    if g.kind == -1:
                        chain[:] = [0, 0]
                        dve.wait_ge(x_loaded, 16)
                        ln_stats_of(x_in, 0, ln_stats)
                        dve.wait_ge(ln_rstd, 1)
                        ln_apply(x_in, xln, 0).then_inc(ln_done, 1)
                        for b in range(GB):
                            ctx_lower(g, b)
                        xT_lower(g)
                        for m in range(2):
                            q_lower(g, 1, m)
                        for h in range(HALF):
                            fold_lower(g, 1, h)
                        keep_qbk(g)
                        total = chain[1]
                        continue
                    if g.kind == 0:
                        chain[:] = [total, 0]
                    elif g.kind == 1:
                        start = total + chain[1]
                        per["loop"] = per_loop = LINKS_PER_GROUP
                        chain[:] = [start + (g.at - 1) * per_loop, 0]
                    elif g.kind == GROUPS - 1:
                        assert chain[1] == per["loop"], chain[1]
                        chain[:] = [start + (GROUPS - 2) * per["loop"], 0]
                    for s in range(STEPS):
                        half, b = divmod(s, GB)
                        if s == 0 and g.cur:
                            wait_freed(dve, g, ("qbk",), -1)
                        if g.cur:
                            peaks(g, s)
                        if half == 1 and g.next:
                            ctx_lower(g, b)
                        if b == 2 and (g.cur if half else g.prev):
                            bank, free = wait_filled(dve, g, ("v", half, 1))
                            for i in range(2):
                                pair = (1 - half) * PAIRS + 2 + i
                                last = nc.vector.tensor_scalar(oT[:, pair, :], bank[:, i * GT:(i + 1) * GT],
                                                               bv[:, pair:pair + 1], None, ALU.add)
                            last.then_inc(free, 1)
                        if s == 3 and g.prev:
                            dve.wait_ge(x1_stored, 16 * g.at)
                            for n in range(TILES):
                                bank, free = wait_filled(dve, g, ("o", n))
                                nc.vector.tensor_tensor(z[:, n, :], bank[:, 0:D], resid[:, n, :], ALU.add).then_inc(free, 1)
                        if s == 6 and g.next:
                            xT_lower(g)
                        if b == 3 and (g.next if half else g.cur):
                            for h in range(HALF):
                                fold_lower(g, half, h)
                        if s == 7 and g.next:
                            keep_qbk(g)
                        if s == 6 and g.prev:
                            both(lambda n: nc.vector.scalar_tensor_tensor(
                                out=z[:, n, :], in0=z[:, n, :], scalar=mv[:, 1, n, 0:1], in1=gamma[:, :],
                                op0=ALU.subtract, op1=ALU.mult), linked=True)
                            both(lambda n: nc.vector.scalar_tensor_tensor(
                                out=z[:, n, :], in0=z[:, n, :], scalar=rstd[:, 1, n:n + 1], in1=x_again[:, n, :],
                                op0=ALU.mult, op1=ALU.add)).then_inc(tail_done, 1)
                        if s == 4 and g.prev:
                            for n in range(TILES):
                                wait_freed(dve, g, ("o", n))
                            ln_stats_of(z, 1, tail_stats)
                        if s == 4 and g.next:
                            dve.wait_ge(x_loaded, 16 * (g.at + 2))
                            ln_stats_of(x_in, 0, ln_stats)
                        if s == 5 and g.prev:
                            dve.wait_ge(x_reloaded, 16 * g.at)
                            both(lambda n: nc.vector.tensor_tensor(x_again[:, n, :], x_again[:, n, :], beta[:, :], ALU.add),
                                 linked=True)
                            dve.wait_ge(tail_rstd, g.at)
                        if (g.cur if s >= 1 else g.prev):
                            for k in range(KC):
                                pT_lower(g, s, k)
                        if b == 2 and (g.next if half else g.cur):
                            for m in range(2):
                                q_lower(g, half, m)
                        if g.cur:
                            normalise(g, s)
                        if s == 4 and g.cur:
                            dve.wait_ge(ln_done, g.at + 1)
                            if g.prev:
                                for n in range(TILES):
                                    wait_freed(dve, g, ("o", n))
                            both(lambda n: nc.vector.tensor_tensor(resid[:, n, :], xln[:, n, :], bo[:, :], ALU.add)
                                 ).then_inc(resid_done, 1)
                        if s == 5 and g.next:
                            dve.wait_ge(ln_rstd, g.at + 2)
                            dve.wait_ge(resid_done, g.at + 1)
                            wait_filled(dve, g, ("xT",), -1)
                            ln_apply(x_in, xln, 0).then_inc(ln_done, 1)

            @block.tensor
            def _(pe):
                pe.wait_ge(weights_in, 32)
                pe.wait_ge(pool_setup, 2)
                wk_raw = wstage[:, 0:2048].rearrange("p (c n) -> p c n", c=DC)
                for j in range(4):
                    for m in range(2):
                        for c in range(DC):
                            pair = 2 * j + m
                            last = nc.tensor.transpose(ring[:, j, (m * DC + c) * P:(m * DC + c + 1) * P],
                                                       wk_raw[:, c, pair * P:(pair + 1) * P], ident[:, :])
                    last.then_inc(setup_T, 1)
                pe.wait_ge(setup_hi, 17)
                pe.wait_ge(setup_lo, 17)

                def exact3(out, pairs):
                    n = 0
                    for (lh, ll), (rh, rl) in pairs:
                        for a, b in ((lh, rh), (lh, rl), (ll, rh)):
                            last = nc.tensor.matmul(out, a, b, start=(n == 0), stop=(n == 3 * len(pairs) - 1))
                            n += 1
                    return last

                def do_scores(g, s):
                    half, b = divmod(s, GB)
                    if b == 0:
                        for h in range(HALF - RING, HALF):
                            if half == 0:
                                wait_freed(pe, g, ("fold", 1, h), -1)
                            else:
                                wait_freed(pe, g, ("fold", 0, h))
                    if half == 0:
                        wait_freed(pe, g, ("ctxT", b), -1)
                    if not (g.kind == 0 and s < 2):
                        pe.wait_ge(exp_done, PAIRS * (STEPS * g.at + s - 1))
                    for p in range(PAIRS):
                        out = scores[:, s % 2, p // 2, (p % 2) * SK:(p % 2 + 1) * SK]
                        last = exact3(out, [((qk_hi[:, c, b, 2 * p:2 * p + 2, :], qk_lo[:, c, b, 2 * p:2 * p + 2, :]),
                                             (ctxT_hi[:, b, c, :], ctxT_lo[:, b, c, :])) for c in range(DC)])
                        if p % 2:
                            last.then_inc(scores_done, 1)

                def do_ctxT(g, b):
                    pe.wait_ge(ctx_in[b], 16 * (g.at + 2))
                    bank, done = bank_for(pe, g, ("ctxT", b))
                    for c in range(DC):
                        for k in range(KC):
                            at = c * SK + k * P
                            last = nc.tensor.transpose(bank[:, at:at + P], ctx_raw[:, b, k, c * P:(c + 1) * P], ident[:, :])
                    last.then_inc(done, 1)

                def do_fold(g, half):
                    for m in range(2):
                        wait_freed(pe, g, ("q", half, m))
                    target = 1 - half
                    for h in range(HALF):
                        bank, done = bank_for(pe, g, ("fold", half, h))
                        for c in range(DC):
                            for n, w in enumerate((wk_hi, wk_lo)):
                                last = nc.tensor.matmul(bank[:, c * GT:(c + 1) * GT],
                                                        w[:, target * HALF + h, c * P:(c + 1) * P], q_st[:, h, :],
                                                        start=(n == 0), stop=(n == 1))
                        last.then_inc(done, 1)

                def do_pc(g, s):
                    b = (s + 2) % GB
                    if s == 0:
                        for k in range(KC):
                            wait_freed(pe, g, ("pt", STEPS - 1, k), -1)
                    else:
                        for k in range(KC):
                            wait_freed(pe, g, ("pt", s - 1, k))
                    if s >= 2:
                        pe.wait_ge(ctx_split, GB * g.at + b + 1)
                    for c in range(DC):
                        bank, done = bank_for(pe, g, ("pc", s, c))
                        at = slice(c * P, (c + 1) * P)
                        exact3(bank, [((ctx_hi[:, b, k, at], ctx_lo[:, b, k, at]), (pT_hi[:, k, :], pT_lo[:, k, :]))
                                      for k in range(KC)]).then_inc(done, 1)

                def do_pT(g, s):
                    pe.wait_ge(probs_done, STEPS * g.at + s)
                    for k in range(KC):
                        bank, done = bank_for(pe, g, ("pt", s, k))
                        for p in range(PAIRS):
                            last = nc.tensor.transpose(bank[:, p * P:(p + 1) * P],
                                                       probs[:, (s - 1) % 2, p, k * P:(k + 1) * P], ident[:, :])
                        last.then_inc(done, 1)

                def do_v(g, half):
                    for c in range(DC):
                        wait_freed(pe, g, ("pc", half * GB + 1, c))
                    for j in range(2):
                        bank, done = bank_for(pe, g, ("v", half, j))
                        for i in range(2):
                            for c in range(DC):
                                for hp in range(2):
                                    h = 4 * j + 2 * i + hp
                                    col = ((1 - half) * HALF + h) * DK
                                    last = nc.tensor.matmul(bank[hp * DK:(hp + 1) * DK, i * GT:(i + 1) * GT],
                                                            wv[:, c, col:col + DK], pc[:, c, h, :],
                                                            start=(c == 0), stop=(c == DC - 1))
                        last.then_inc(done, 1)

                def do_o(g):
                    for j in range(2):
                        wait_freed(pe, g, ("v", 0, j))
                    for n in range(TILES):
                        bank, done = bank_for(pe, g, ("o", n))
                        for m in range(HALF):
                            last = nc.tensor.matmul(bank[:, 0:D], oT[:, m, n * P:(n + 1) * P], wo[:, m, :],
                                                    start=(m == 0), stop=(m == HALF - 1))
                        last.then_inc(done, 1)

                def do_xT(g):
                    pe.wait_ge(ln_done, g.at + 2)
                    bank, done = bank_for(pe, g, ("xT",))
                    for c in range(DC):
                        for n in range(TILES):
                            last = nc.tensor.transpose(bank[:, c * GT + n * P:c * GT + (n + 1) * P],
                                                       xln[:, n, c * P:(c + 1) * P], ident[:, :])
                    last.then_inc(done, 1)

                def do_qbk(g):
                    bank, done = bank_for(pe, g, ("qbk",))
                    for n in range(TILES):
                        at = slice(n * P, (n + 1) * P)
                        last = exact3(bank[:, n * HEADS:(n + 1) * HEADS],
                                      [((xT_hi[:, c, at], xT_lo[:, c, at]), (wqb_hi[:, c, :], wqb_lo[:, c, :]))
                                       for c in range(DC)])
                    last.then_inc(done, 1)

                def do_q(g, half):
                    target = 1 - half
                    if half == 1:
                        wait_freed(pe, g, ("xT",))
                    for m in range(2):
                        bank, done = bank_for(pe, g, ("q", half, m))
                        for i in range(2):
                            col = (target * PAIRS + 2 * m + i) * P
                            last = exact3(bank[:, i * GT:(i + 1) * GT],
                                          [((wq_hi[:, c, col:col + P], wq_lo[:, c, col:col + P]),
                                            (xT_hi[:, c, :], xT_lo[:, c, :])) for c in range(DC)])
                        last.then_inc(done, 1)

                for g in turns(pe):
                    if g.kind == -1:
                        for b in range(GB):
                            do_ctxT(g, b)
                        do_xT(g)
                        do_q(g, 1)
                        do_fold(g, 1)
                        pe.wait_ge(wqb_done, 1)
                        do_qbk(g)
                        continue
                    for s in range(STEPS):
                        half, b = divmod(s, GB)
                        if g.cur:
                            do_scores(g, s)
                        if half == 1 and g.next:
                            do_ctxT(g, b)
                        if b == 2 and (g.cur if half else g.prev):
                            do_v(g, half)
                        if s == 3 and g.prev:
                            do_o(g)
                        if s == 6 and g.next:
                            do_xT(g)
                        if (g.cur if s >= 2 else g.prev):
                            do_pc(g, s)
                        if b == 3 and (g.next if half else g.cur):
                            do_fold(g, half)
                        if s == 7 and g.next:
                            do_qbk(g)
                        if (g.cur if s >= 1 else g.prev):
                            do_pT(g, s)
                        if b == 2 and (g.next if half else g.cur):
                            do_q(g, half)


TOKENS = BATCH * SQ
NT = TOKENS // P
SH = 16
HD = D // SH
ROPE_BASE = 100000.0
HEAD_SCALE = float(HD) ** -0.5
SRING = 5
LINKS_PER_PAIR = 16


def rope_tables():
    pairs = HD // 2
    freqs = (1.0 / ROPE_BASE ** (np.arange(pairs, dtype=np.float32) / pairs)).astype(np.float32)
    angles = np.outer(np.arange(SQ, dtype=np.float32), freqs).astype(np.float32)
    cos, sin = np.cos(angles), np.sin(angles)
    table = np.concatenate([cos, cos, -sin, sin], axis=1)
    odd = (np.arange(P) // HD % 2)[:, None]
    return np.concatenate([np.concatenate([table, table], axis=0), 1 - odd, odd], axis=1).astype(np.float32)


class Pair:

    def __init__(self, at, kind):
        self.at, self.kind = at, kind

    def has(self, s, off):
        return self.kind == 1 or 0 <= 2 * self.kind + s + off < NT

    def tile(self, s, off=0):
        return 2 * self.at + s + off


def pair_turns(eng):
    yield Pair(-2, -2)
    yield Pair(-1, -1)
    yield Pair(0, 0)
    with eng.Fori(1, NT // 2 - 2) as g:
        yield Pair(g, 1)
    yield Pair(NT // 2 - 2, NT // 2 - 2)
    yield Pair(NT // 2 - 1, NT // 2 - 1)
    yield Pair(NT // 2, NT // 2)


def pair_order(kind):
    g = Pair(None, kind)
    out = []
    for s in range(2):
        if g.has(s, 2):
            out.append(("xT", s))
        if g.has(s, 1):
            out.append(("qkT", s))
        if g.has(s, -1):
            out += [("pT", s, 0), ("pT", s, 1)]
        if g.has(s, 1):
            out.append(("v", s))
        if g.has(s, 2):
            out.append(("qk", s))
        if g.has(s, -2):
            out.append(("x3T", s))
        if g.has(s, -1):
            out += [("o", s), ("y", s)]
        if g.has(s, -2):
            out.append(("gate", s))
    return out


def self_attention(nc, t, x1_dram, x2_dram, xl_dram, logits, load_ahead=None):
    with ExitStack() as ctx:
        def sb(name, shape, dt=F32):
            return ctx.enter_context(nc.sbuf_tensor("s_" + name, shape, dt))

        def sem(name):
            return ctx.enter_context(nc.semaphore("s_" + name))

        ident = sb("ident", [P, P])
        w_raw = sb("w_raw", [P, 4, DC, D])
        w_hi = sb("w_hi", [P, DC, 3 * D], F32R)
        w_lo = sb("w_lo", [P, DC, 3 * D], F32R)
        woT = sb("woT", [P, DC, D])
        wg = sb("wg", [P, DC, 8])
        table = sb("table", [P, 2 * HD + 2])
        bqk = sb("bqk", [P, 2 * D])
        turned_b = sb("turned_b", [P, 2 * D])
        bvp = sb("bvp", [P, DC])
        bo = sb("bo", [P, D])
        power = sb("power", [P, 1])
        x1 = sb("x1", [P, 2, D])
        x1_again = sb("x1_again", [P, 2, D])
        xn = sb("xn", [P, D])
        stats = sb("stats", [P, 2, 6])
        mv = sb("mv", [P, 2, 2])
        rstd = sb("rstd", [P, 2])
        xT_hi = sb("xT_hi", [P, 2, DC, P], F32R)
        xT_lo = sb("xT_lo", [P, 2, DC, P], F32R)
        turned = sb("turned", [P, 2 * D])
        swapped = sb("swapped", [P, 2 * D])
        qz = sb("qz", [P, 2, DC, P])
        kbd = sb("kbd", [P, DC, 2, 4, SQ])
        vbd = sb("vbd", [P, 2, 2, 2, 4, 32])
        probs = sb("probs", [P, 1024])
        peak = sb("peak", [P, SH])
        shifted = sb("shifted", [P, 1024])
        rsum = sb("rsum", [P, SH])
        rinv = sb("rinv", [P, SH])
        pT = sb("pT", [P, DC, 512])
        oT = sb("oT", [P, DC, P])
        x2 = sb("x2", [P, 2, D])
        xl = sb("xl", [P, 2, D])
        x3T = sb("x3T", [P, DC, P])

        scores = ctx.enter_context(nc.psum_tensor("s_scores", [P, 2, 512], F32))
        ring = ctx.enter_context(nc.psum_tensor("s_ring", [P, SRING, 512], F32))

        weights_in = sem("weights_in")
        small_in = sem("small_in")
        pool_setup = sem("pool_setup")
        setup_T = sem("setup_T")
        setup_hi = sem("setup_hi")
        setup_lo = sem("setup_lo")
        x1_in = [sem(f"x1_in{i}") for i in range(2)]
        x1_reloaded = [sem(f"x1_reloaded{i}") for i in range(2)]
        filled = [sem(f"filled{k}") for k in range(SRING)]
        freed = [sem(f"freed{k}") for k in range(SRING)]
        hi_done = sem("hi_done")
        ln_stats = sem("ln_stats")
        ln_rstd = sem("ln_rstd")
        ln_done = sem("ln_done")
        l3_stats = sem("l3_stats")
        l3_rstd = sem("l3_rstd")
        l3_done = sem("l3_done")
        cos_done = sem("cos_done")
        biased = sem("biased")
        turn_done = sem("turn_done")
        scores_done = sem("scores_done")
        shifted_done = sem("shifted_done")
        exp_done = sem("exp_done")
        rinv_done = sem("rinv_done")
        probs_done = sem("probs_done")
        x1_biased = sem("x1_biased")
        x2_stored = [sem(f"x2_stored{i}") for i in range(2)]
        xl_stored = [sem(f"xl_stored{i}") for i in range(2)]
        dve_step = sem("dve_step")
        pool_step = sem("pool_step")
        dve_past = sem("dve_past")

        ring_turns = Turns(pair_order, -2, NT // 2, 3)
        assert ring_turns.loop % SRING == 0

        def place(g, key, pairs_on=0):
            if isinstance(g.at, int):
                c, f = ring_turns.index(g.at + pairs_on, key)
            else:
                c, f = ring_turns.index(g.at, key)
                c += ring_turns.loop * pairs_on
            return c % SRING, (c // SRING + 1, f // SRING)

        seen = {}

        def reach(eng, g, semaphores, k, count):
            c, f = count
            at = (id(eng), semaphores is filled, k)
            if seen.get(at, (None, 0))[0] is g and seen[at][1] >= c:
                return
            seen[at] = (g, c)
            eng.wait_ge(semaphores[k], c + f * g.at if f else c)

        def wait_filled(eng, g, key, pairs_on=0):
            k, count = place(g, key, pairs_on)
            reach(eng, g, filled, k, count)
            return ring[:, k, :], freed[k]

        def wait_freed(eng, g, key, pairs_on=0):
            k, count = place(g, key, pairs_on)
            reach(eng, g, freed, k, count)

        def bank_for(eng, g, key):
            k, (c, f) = place(g, key)
            if f or c > 1:
                reach(eng, g, freed, k, (c - 1, f))
            return ring[:, k, :], filled[k]

        def before(g, s, key):
            return ((key[0], s - 1, *key[2:]), 0) if s else ((key[0], 1, *key[2:]), -1)

        x1_tiles = x1_dram.rearrange("(n p) d -> n p d", p=P)
        x2_tiles = x2_dram.rearrange("(n p) d -> n p d", p=P)
        xl_tiles = xl_dram[0:TOKENS, :].rearrange("(n p) d -> n p d", p=P)

        def tile_of(tiles, n):
            return tiles[n] if isinstance(n, int) else tiles[bass.ds(n, 1)].rearrange("a p d -> (a p) d")

        with nc.Block() as block:
            @block.sync
            def _(sp):
                for i, name in enumerate(("Wq", "Wk", "Wv")):
                    sp.dma_start(w_raw[:, i], t[f"L0_attn_{name}"].rearrange("(c p) n -> p c n", p=P)).then_inc(weights_in, 16)
                wo = t["L0_attn_Wo"].rearrange("(c p) (m u e d) -> c m e p u d", p=P, m=DC, e=2, d=HD)
                for c in range(DC):
                    for m in range(DC):
                        for e in range(2):
                            at = m * P + e * SQ
                            sp.dma_start(w_raw[:, 3, c, at:at + SQ].rearrange("p (u d) -> p u d", d=HD), wo[c, m, e]
                                         ).then_inc(weights_in, 16)
                sp.dma_start(table[:, :], t["rope"]).then_inc(small_in, 16)
                sp.dma_start(bqk[:, 0:D], t["L0_attn_bq"].partition_broadcast(P)).then_inc(small_in, 16)
                sp.dma_start(bqk[:, D:], t["L0_attn_bk"].partition_broadcast(P)).then_inc(small_in, 16)
                sp.dma_start(bo[:, :], t["L0_attn_bo"].partition_broadcast(P)).then_inc(small_in, 16)
                sp.dma_start(wg[:, :, :], t["L0_ffn_Wg"].rearrange("(c p) n -> p c n", p=P)).then_inc(small_in, 16)
                for e in range(2):
                    for r in range(4):
                        at = (4 * e + r) * HD
                        src = t["L0_attn_bv"].rearrange("(m r e d) -> e r d m", m=2, r=4, e=2)[e, r]
                        sp.dma_start(bvp[at:at + HD, :], src, allow_slow_non_contiguous=True).then_inc(small_in, 16)
                for s in range(2):
                    sp.sem_inc(xl_stored[s], 16)
                    sp.sem_inc(x2_stored[s], 16)
                for g in pair_turns(sp):
                    for s in range(2):
                        if g.has(s, 4):
                            if g.has(s, 2):
                                sp.wait_ge(ln_done, g.tile(s, 3))
                            sp.dma_start(x1[:, s, :], tile_of(x1_tiles, g.tile(s, 4))).then_inc(x1_in[s], 16)
                        if g.has(s, 0):
                            if g.has(s, -2):
                                sp.wait_ge(l3_stats, g.tile(s, -1))
                            sp.dma_start(x1_again[:, s, :], tile_of(x1_tiles, g.tile(s))).then_inc(x1_reloaded[s], 16)
                        if g.has(s, -2):
                            sp.wait_ge(l3_done, g.tile(s, -1))
                            sp.dma_start(tile_of(xl_tiles, g.tile(s, -2)), xl[:, s, :]).then_inc(xl_stored[s], 16)
                            sp.dma_start(tile_of(x2_tiles, g.tile(s, -2)), x2[:, s, :]).then_inc(x2_stored[s], 16)
                for s in range(2):
                    sp.wait_ge(xl_stored[s], 16 * (NT // 2 + 1))
                    sp.wait_ge(x2_stored[s], 16 * (NT // 2 + 1))

            def rotate(src, out_cos, out_sin, done):
                def heads(x):
                    return x.rearrange("p (h d) -> p h d", d=HD)

                def angles(at, n):
                    return table[:, at:at + n].unsqueeze(1).broadcast_to([P, 2 * SH, n])

                h = HD // 2
                done[0](nc.vector.tensor_tensor(heads(out_cos), heads(src), angles(0, HD), ALU.mult))
                done[1](nc.vector.tensor_tensor(heads(out_sin)[:, :, 0:h], heads(src)[:, :, h:HD], angles(HD, h), ALU.mult))
                done[2](nc.vector.tensor_tensor(heads(out_sin)[:, :, h:HD], heads(src)[:, :, 0:h], angles(HD + h, h), ALU.mult))

            @block.gpsimd
            def _(pool):
                nc.gpsimd.memset(ident[:, :], 0.0).then_inc(pool_step, 1)
                nc.gpsimd.memset(power[:, :], -0.5).then_inc(pool_setup, 1)
                nc.gpsimd.memset(kbd[:, :, :, :, :], 0.0).then_inc(pool_setup, 1)
                nc.gpsimd.memset(vbd[:, :, :, :, :, :], 0.0).then_inc(pool_setup, 1)
                pool.wait_ge(pool_step, 1)
                nc.gpsimd.affine_select(out=ident[:, :], in_=ident[:, :], compare_op=ALU.not_equal, fill=1.0,
                                        base=0, pattern=[[-1, P]], channel_multiplier=1).then_inc(pool_setup, 1)
                pool.wait_ge(pool_setup, 4)
                if load_ahead:
                    pool.wait_ge(weights_in, 16 * 11)
                    load_ahead(pool)

                def rsqrt(which, ready, done, nth):
                    pool.wait_ge(ready, nth)
                    nc.gpsimd.tensor_tensor(rstd[:, which:which + 1], mv[:, which, 1:2], power[:, :],
                                            ALU.pow).then_inc(done, 1)

                for g in pair_turns(pool):
                    for s in range(2):
                        if g.has(s, -2):
                            rsqrt(1, l3_stats, l3_rstd, g.tile(s, -1))
                        if g.has(s, 3):
                            rsqrt(0, ln_stats, ln_rstd, g.tile(s, 4))
                        if g.has(s, -1):
                            o = (s + 1) % 2
                            pool.wait_ge(x1_reloaded[o], 16 * (g.at + (1 if s else 0)))
                            nc.gpsimd.tensor_tensor(x1_again[:, o, :], x1_again[:, o, :], bo[:, :], ALU.add
                                                    ).then_inc(x1_biased, 1)
                        if g.has(s, 2):
                            pool.wait_ge(cos_done, g.tile(s, 3))
                            nc.gpsimd.tensor_tensor(turned[:, :], turned[:, :], turned_b[:, :], ALU.add).then_inc(biased, 1)
                            wait_freed(pool, g, ("qk", s))
                            pool.wait_ge(biased, g.tile(s, 3))
                            nc.gpsimd.tensor_tensor(turned[:, :], turned[:, :], swapped[:, :], ALU.add).then_inc(turn_done, 1)
                        if g.has(s, 0):
                            pool.wait_ge(rinv_done, g.tile(s, 1))
                            nc.gpsimd.tensor_tensor(probs[:, :].rearrange("p (h k) -> p h k", k=SQ),
                                                    probs[:, :].rearrange("p (h k) -> p h k", k=SQ),
                                                    rinv[:, :].unsqueeze(2).broadcast_to([P, SH, SQ]),
                                                    ALU.mult).then_inc(probs_done, 1)

            @block.scalar
            def _(act):
                act.wait_ge(small_in, 16 * 13)
                act.wait_ge(pool_setup, 4)
                for j in range(4):
                    act.wait_ge(setup_T, j + 1)
                    src = ring[:, j, :].rearrange("p (c n) -> p c n", c=DC)
                    out = w_hi[:, :, j * D:(j + 1) * D] if j < 3 else woT[:, :, :]
                    nc.scalar.activation(out, src, ACT.Identity).then_inc(setup_hi, 1)

                def copy(out, src, **kw):
                    return nc.scalar.activation(out, src, ACT.Identity, **kw)

                for g in pair_turns(act):
                    for s in range(2):
                        if g.has(s, 2):
                            bank, _ = wait_filled(act, g, ("xT", s))
                            copy(xT_hi[:, s], bank[:, 0:D].rearrange("p (c n) -> p c n", c=DC)).then_inc(hi_done, 1)
                        if g.has(s, 1):
                            bank, free = wait_filled(act, g, ("qkT", s))
                            for e in range(2):
                                copy(qz[:, e], bank[:, 0:D].rearrange("p (m n) -> p m n", m=DC),
                                     scale=table[:, 2 * HD + e:2 * HD + e + 1])
                            for r in range(4):
                                rows = slice(32 * r, 32 * r + 32)
                                last = copy(kbd[rows, :, :, r, :],
                                            bank[rows, D:2 * D].rearrange("p (m b k) -> p m b k", m=DC, b=2))
                            last.then_inc(free, 1)
                        if g.has(s, -1):
                            for m in range(2):
                                bank, free = wait_filled(act, g, ("pT", s, m))
                                copy(pT[:, m, :], bank).then_inc(free, 1)
                        if g.has(s, 0):
                            act.wait_ge(shifted_done, 2 * g.tile(s, 1))
                            nc.scalar.activation(probs[:, :], shifted[:, :], ACT.Exp, scale=HEAD_SCALE).then_inc(exp_done, 1)
                        if g.has(s, -2):
                            bank, free = wait_filled(act, g, ("x3T", s))
                            copy(x3T[:, :, :], bank[:, 0:D].rearrange("p (c n) -> p c n", c=DC)).then_inc(free, 1)
                        if g.has(s, -1):
                            bank, free = wait_filled(act, g, ("o", s))
                            for m in range(2):
                                last = copy(oT[:, m, :], bank[:, m * P:(m + 1) * P], bias=bvp[:, m:m + 1])
                            last.then_inc(free, 1)
                        if g.has(s, 1):
                            bank, free = wait_filled(act, g, ("v", s))
                            for b in range(2):
                                rows = slice(b * SQ, (b + 1) * SQ)
                                src = bank[rows, 0:D].rearrange("p (u i e d) -> p e u i d", u=4, i=2, e=2)
                                for i in range(2):
                                    last = copy(vbd[i * SQ:(i + 1) * SQ, (s + 1) % 2, b, :, :, i * HD:(i + 1) * HD],
                                                src[:, :, :, i, :])
                            last.then_inc(free, 1)

            @block.vector
            def _(dve):
                chain = [0, 0]

                def link(ins):
                    chain[1] += 1
                    ins.then_inc(dve_step, 1)
                    dve.wait_ge(dve_step, chain[0] + chain[1])

                def step(ins):
                    chain[1] += 1
                    return ins.then_inc(dve_step, 1)

                for j in range(3):
                    dve.wait_ge(setup_hi, j + 1)
                    nc.vector.tensor_tensor(w_lo[:, :, j * D:(j + 1) * D], ring[:, j, :].rearrange("p (c n) -> p c n", c=DC),
                                            w_hi[:, :, j * D:(j + 1) * D], ALU.subtract).then_inc(setup_lo, 1)
                dve.wait_ge(small_in, 16 * 13)
                rotate(bqk[:, :], turned_b[:, :], swapped[:, :], (step, step, link))
                link(nc.vector.tensor_tensor(turned_b[:, :], turned_b[:, :], swapped[:, :], ALU.add))

                def ln_of(src, which, ready):
                    link(nc.vector.bn_stats(stats[:, which, :], src))
                    dve.sem_inc(dve_past, 1)
                    link(nc.vector.bn_aggr(mv[:, which, :], stats[:, which, :]))
                    nc.vector.tensor_scalar(mv[:, which, 1:2], mv[:, which, 1:2], EPS, None, ALU.add).then_inc(ready, 1)

                for g in pair_turns(dve):
                    if g.kind <= 0:
                        chain[:] = [chain[0] + chain[1], 0]
                    elif g.kind == 1:
                        start = chain[0] + chain[1]
                        chain[:] = [start + (g.at - 1) * LINKS_PER_PAIR, 0]
                    else:
                        if g.kind == NT // 2 - 2:
                            assert chain[1] == LINKS_PER_PAIR, chain[1]
                            chain[:] = [start + (NT // 2 - 3) * LINKS_PER_PAIR, 0]
                        else:
                            chain[:] = [chain[0] + chain[1], 0]
                    for s in range(2):
                        if g.has(s, 2):
                            dve.wait_ge(ln_rstd, g.tile(s, 3))
                            nc.vector.tensor_scalar(xn[:, :], x1[:, s, :], mv[:, 0, 0:1], rstd[:, 0:1],
                                                    ALU.subtract, ALU.mult).then_inc(ln_done, 1)
                        if g.has(s, 0):
                            dve.wait_ge(scores_done, g.tile(s, 1))
                            for m in range(2):
                                add = step if m == 0 else link
                                add(nc.vector.tensor_reduce(peak[:, 8 * m:8 * m + 8],
                                                            scores[:, m, :].rearrange("p (h k) -> p h k", k=SQ), AX_X, ALU.max))
                        if g.has(s, 2):
                            k, _ = place(g, ("xT", s))
                            dve.wait_ge(hi_done, g.tile(s, 3))
                            nc.vector.tensor_tensor(xT_lo[:, s], ring[:, k, 0:D].rearrange("p (c n) -> p c n", c=DC),
                                                    xT_hi[:, s], ALU.subtract).then_inc(freed[k], 1)
                        if g.has(s, 0):
                            for m in range(2):
                                nc.vector.tensor_tensor(shifted[:, 512 * m:512 * m + 512].rearrange("p (h k) -> p h k", k=SQ),
                                                        scores[:, m, :].rearrange("p (h k) -> p h k", k=SQ),
                                                        peak[:, 8 * m:8 * m + 8].unsqueeze(2).broadcast_to([P, 8, SQ]),
                                                        ALU.subtract).then_inc(shifted_done, 1)
                        if g.has(s, -2):
                            dve.wait_ge(l3_rstd, g.tile(s, -1))
                            if g.has(s, -4):
                                dve.wait_ge(xl_stored[s], 16 * g.at)
                            nc.vector.tensor_scalar(xl[:, s, :], x2[:, s, :], mv[:, 1, 0:1], rstd[:, 1:2],
                                                    ALU.subtract, ALU.mult).then_inc(l3_done, 1)
                        if g.has(s, 3):
                            o = (s + 1) % 2
                            dve.wait_ge(x1_in[o], 16 * (g.at + (s + 3) // 2 + 1))
                            ln_of(x1[:, o, :], 0, ln_stats)
                        if g.has(s, 2):
                            bank, free = wait_filled(dve, g, ("qk", s))
                            if g.has(s, 1):
                                dve.wait_ge(turn_done, g.tile(s, 2))
                            rotate(bank, turned[:, :], swapped[:, :],
                                   (lambda i: i.then_inc(cos_done, 1), step, lambda i: i.then_inc(free, 1)))
                        if g.has(s, 0):
                            dve.wait_ge(exp_done, g.tile(s, 1))
                            link(nc.vector.tensor_reduce(rsum[:, :], probs[:, :].rearrange("p (h k) -> p h k", k=SQ),
                                                         AX_X, ALU.add))
                            nc.vector.reciprocal(rinv[:, :], rsum[:, :]).then_inc(rinv_done, 1)
                        if g.has(s, -1):
                            o = (s + 1) % 2
                            if g.has(s, -3):
                                dve.wait_ge(x2_stored[o], 16 * (g.at + s))
                            dve.wait_ge(x1_biased, g.tile(s))
                            bank, free = wait_filled(dve, g, ("y", s))
                            nc.vector.tensor_tensor(x2[:, o, :], bank[:, 0:D], x1_again[:, o, :], ALU.add).then_inc(free, 1)
                            k, count = place(g, ("y", s))
                            reach(dve, g, freed, k, count)
                            ln_of(x2[:, o, :], 1, l3_stats)
                        if g.has(s, -2):
                            bank, free = wait_filled(dve, g, ("gate", s))
                            out = logits[:, g.tile(s, -2), :] if isinstance(g.at, int) else \
                                logits[:, bass.ds(g.tile(s, -2), 1), :].rearrange("p a e -> p (a e)")
                            nc.vector.tensor_copy(out, bank[:, 0:8]).then_inc(free, 1)

            @block.tensor
            def _(pe):
                pe.wait_ge(weights_in, 16 * 11)
                pe.wait_ge(pool_setup, 4)
                for j in range(4):
                    for c in range(DC):
                        for m in range(DC):
                            last = nc.tensor.transpose(ring[:, j, c * D + m * P:c * D + (m + 1) * P],
                                                       w_raw[:, j, m, c * P:(c + 1) * P], ident[:, :])
                    last.then_inc(setup_T, 1)
                pe.wait_ge(setup_hi, 4)
                pe.wait_ge(setup_lo, 3)

                def exact3(out, pairs):
                    n = 0
                    for (lh, ll), (rh, rl) in pairs:
                        for a, b in ((lh, rh), (lh, rl), (ll, rh)):
                            last = nc.tensor.matmul(out, a, b, start=(n == 0), stop=(n == 3 * len(pairs) - 1))
                            n += 1
                    return last

                for g in pair_turns(pe):
                    for s in range(2):
                        if g.has(s, 0):
                            wait_freed(pe, g, *before(g, s, ("qkT", s)))
                            if g.has(s, -1):
                                pe.wait_ge(shifted_done, 2 * g.tile(s))
                            for m in range(2):
                                for e in range(2):
                                    for b in range(2):
                                        last = nc.tensor.matmul(scores[b * SQ:(b + 1) * SQ, m, e * D:(e + 1) * D],
                                                                qz[:, e, m, b * SQ:(b + 1) * SQ],
                                                                kbd[:, m, b, :, :], start=True, stop=True)
                            last.then_inc(scores_done, 1)
                        if g.has(s, 2):
                            pe.wait_ge(ln_done, g.tile(s, 3))
                            bank, done = bank_for(pe, g, ("xT", s))
                            for c in range(DC):
                                last = nc.tensor.transpose(bank[:, c * P:(c + 1) * P], xn[:, c * P:(c + 1) * P], ident[:, :])
                            last.then_inc(done, 1)
                        if g.has(s, 1):
                            pe.wait_ge(turn_done, g.tile(s, 2))
                            bank, done = bank_for(pe, g, ("qkT", s))
                            for c in range(4):
                                last = nc.tensor.transpose(bank[:, c * P:(c + 1) * P], turned[:, c * P:(c + 1) * P], ident[:, :])
                            last.then_inc(done, 1)
                        if g.has(s, -1):
                            pe.wait_ge(probs_done, g.tile(s))
                            for m in range(2):
                                bank, done = bank_for(pe, g, ("pT", s, m))
                                for c in range(4):
                                    at = 512 * m + c * P
                                    last = nc.tensor.transpose(bank[:, c * P:(c + 1) * P], probs[:, at:at + P], ident[:, :])
                                last.then_inc(done, 1)
                        if g.has(s, 1):
                            bank, done = bank_for(pe, g, ("v", s))
                            o = (s + 1) % 2
                            exact3(bank[:, 0:D], [((xT_hi[:, o, c, :], xT_lo[:, o, c, :]),
                                                   (w_hi[:, c, 2 * D:], w_lo[:, c, 2 * D:])) for c in range(DC)]
                                   ).then_inc(done, 1)
                        if g.has(s, 2):
                            wait_freed(pe, g, ("xT", s))
                            bank, done = bank_for(pe, g, ("qk", s))
                            exact3(bank, [((xT_hi[:, s, c, :], xT_lo[:, s, c, :]),
                                           (w_hi[:, c, 0:2 * D], w_lo[:, c, 0:2 * D])) for c in range(DC)]).then_inc(done, 1)
                        if g.has(s, -2):
                            pe.wait_ge(l3_done, g.tile(s, -1))
                            bank, done = bank_for(pe, g, ("x3T", s))
                            for c in range(DC):
                                last = nc.tensor.transpose(bank[:, c * P:(c + 1) * P], xl[:, s, c * P:(c + 1) * P], ident[:, :])
                            last.then_inc(done, 1)
                        if g.has(s, -1):
                            for m in range(2):
                                wait_freed(pe, g, ("pT", s, m))
                            wait_freed(pe, g, ("v", s), -1)
                            bank, done = bank_for(pe, g, ("o", s))
                            for m in range(2):
                                for b in range(2):
                                    for e in range(2):
                                        for r in range(2):
                                            j = 2 * e + r
                                            last = nc.tensor.matmul(bank[32 * j:32 * j + 32, m * P + b * SQ:m * P + (b + 1) * SQ],
                                                                    vbd[:, (s + 1) % 2, b, e, 2 * m + r, :],
                                                                    pT[:, m, j * P + b * SQ:j * P + (b + 1) * SQ],
                                                                    start=True, stop=True, tile_position=(0, 32 * j))
                            last.then_inc(done, 1)
                            wait_freed(pe, g, ("o", s))
                            bank, done = bank_for(pe, g, ("y", s))
                            for m in range(DC):
                                last = nc.tensor.matmul(bank[:, 0:D], oT[:, m, :], woT[:, m, :],
                                                        start=(m == 0), stop=(m == DC - 1))
                            last.then_inc(done, 1)
                        if g.has(s, -2):
                            wait_freed(pe, g, ("x3T", s))
                            bank, done = bank_for(pe, g, ("gate", s))
                            for c in range(DC):
                                last = nc.tensor.matmul(bank[:, 0:8], x3T[:, c, :], wg[:, c, :],
                                                        start=(c == 0), stop=(c == DC - 1))
                            last.then_inc(done, 1)


E = 8
TOP = 2
F = 512
FC = F // P
SHARED = 1
OUT_SCALE = 1.0 / (SHARED + TOP)
RT = TOP * TOKENS // P + E
SLOTS = RT * P
OUT_ROWS = TOKENS + P
U = 8
GATHERED = 4
YB = 4
assert RT % U == 0


def empty_slots(sp, table_dram, xl_dram, out, empty, zeros, filled):
    sp.dma_start(table_dram.rearrange("(p j) c -> p j c", p=P), empty[:, :, :]).then_inc(filled, 16)
    sp.dma_start(xl_dram[TOKENS:OUT_ROWS, :], zeros[:, :]).then_inc(filled, 16)
    sp.dma_start(out[TOKENS:OUT_ROWS, :], zeros[:, :]).then_inc(filled, 16)


class Turn:

    def __init__(self, at, first=False, last=False):
        self.at, self.first, self.last = at, first, last


def load_experts(sp, t, experts, loaded):
    w1, w3, w2 = experts
    for tile, name in ((w1, "We1"), (w3, "We3"), (w2, "We2")):
        for e in range(E):
            sp.dma_start(tile[:, e].bitcast(F32), t[f"L0_ffn_{name}"][e].rearrange("(c p) n -> p c n", p=P)).then_inc(loaded, 16)


def shared_expert(nc, t, x2_dram, xl_dram, table_dram, out, logits, slots_empty, expert_of):
    with ExitStack() as ctx:
        def sb(name, shape, dt=F32):
            return ctx.enter_context(nc.sbuf_tensor("f_" + name, shape, dt))

        def sem(name):
            return ctx.enter_context(nc.semaphore("f_" + name))

        ident = sb("ident", [P, P])
        before = sb("before", [P, P])
        ones = sb("ones", [P, P])
        back = sb("back", [P, NT, E])
        carry = sb("carry", [P, E, NT])
        tiles_i = sb("tiles_i", [P, RT, E])
        top = sb("top", [P, TOP, NT])
        hot = sb("hot", [P, TOP, NT, E])
        rest = sb("rest", [P, NT, E])
        work = sb("work", [P, NT, E])
        gates = sb("gates", [P, NT, E])
        both = sb("both", [P, NT, E])
        rank = sb("rank", [P, TOP, NT])
        norm = sb("norm", [P, NT])
        totals = sb("totals", [P, E, NT])
        upto = sb("upto", [P, E, NT])
        padded = sb("padded", [P, E])
        padded_i = sb("padded_i", [P, E], I32)
        ends = sb("ends", [P, E])
        starts = sb("starts", [P, E])
        compare = sb("compare", [P, RT, E])
        owner = sb("owner", [P, RT])
        slot = sb("slot", [P, TOP, NT])
        slot_i = sb("slot_i", [P, TOP, NT], U32)
        slot_r = sb("slot_r", [P, TOP, NT], I32)
        slot_p = sb("slot_p", [P, TOP, NT], I32)
        entry = sb("entry", [P, TOP, NT, 2])
        w1_raw = sb("w1_raw", [P, DC, F])
        w3_raw = sb("w3_raw", [P, DC, F])
        w2_raw = sb("w2_raw", [P, FC, D])
        w13_hi = sb("w13_hi", [P, 2, DC, F], F32R)
        w13_lo = sb("w13_lo", [P, 2, DC, F], F32R)
        w2_hi = sb("w2_hi", [P, FC, D], F32R)
        w2_lo = sb("w2_lo", [P, FC, D], F32R)
        x = sb("x", [P, 2, D])
        x2 = sb("x2", [P, 2, D])
        xT_hi = sb("xT_hi", [P, 2, DC, P], F32R)
        xT_lo = sb("xT_lo", [P, 2, DC, P], F32R)
        act1 = sb("act1", [P, 2, F])
        h = sb("h", [P, 2, F])
        hT_hi = sb("hT_hi", [P, FC, P], F32R)
        hT_lo = sb("hT_lo", [P, FC, P], F32R)
        y = sb("y", [P, 2, D])

        def ps(name, n):
            return ctx.enter_context(nc.psum_tensor("f_" + name, [P, n, 512], F32))

        pT = ps("pT", 1)
        p1_, p3_ = ps("p1", 2), ps("p3", 2)
        phT = ps("phT", 1)
        py = ps("py", 1)
        pr = ps("pr", 1)[:, 0, :].rearrange("p (j n) -> p j n", j=2)

        weights_in = sem("weights_in")
        pool_setup = sem("pool_setup")
        w_hi_done = sem("w_hi_done")
        w_lo_done = sem("w_lo_done")
        x_in = [sem(f"x_in{i}") for i in range(2)]
        x2_in = [sem(f"x2_in{i}") for i in range(2)]
        xT_done = sem("xT_done")
        xT_hi_done = sem("xT_hi_done")
        xT_lo_done = sem("xT_lo_done")
        h1_done = sem("h1_done")
        h3_done = sem("h3_done")
        silu_done = sem("silu_done")
        h_done = sem("h_done")
        hT_done = sem("hT_done")
        hT_hi_done = sem("hT_hi_done")
        hT_lo_done = sem("hT_lo_done")
        y_done = sem("y_done")
        y_out = sem("y_out")
        stored = [sem(f"stored{i}") for i in range(2)]
        step = sem("step")
        pool_step = sem("pool_step")
        exp_done = sem("exp_done")
        chosen = sem("chosen")
        counted = sem("counted")
        routed = sem("routed")
        sent = sem("sent")

        x_tiles = xl_dram[0:TOKENS, :].rearrange("(n p) d -> n p d", p=P)
        x2_tiles = x2_dram.rearrange("(n p) d -> n p d", p=P)
        out_tiles = out[0:TOKENS, :].rearrange("(n p) d -> n p d", p=P)

        def tile_of(tiles, n):
            return tiles[n] if isinstance(n, int) else tiles[bass.ds(n, 1)].rearrange("a p d -> (a p) d")

        def column(tile, k, n):
            return tile[:, k, n:n + 1] if isinstance(n, int) else tile[:, k, bass.ds(n, 1)]

        def ahead(eng):
            yield Turn(0, first=True)
            with eng.Fori(1, NT // 2 - 1) as g:
                yield Turn(g)
            yield Turn(NT // 2 - 1, last=True)

        with nc.Block() as block:
            @block.sync
            def _(sp):
                for tile, name in ((w1_raw, "Ws1"), (w3_raw, "Ws3"), (w2_raw, "Ws2")):
                    sp.dma_start(tile[:, :, :], t[f"L0_ffn_{name}"].rearrange("(c p) n -> p c n", p=P)).then_inc(weights_in, 16)
                for s in range(2):
                    sp.dma_start(x[:, s, :], x_tiles[s]).then_inc(x_in[s], 16)
                    sp.dma_start(x2[:, s, :], x2_tiles[s]).then_inc(x2_in[s], 16)
                for g in ahead(sp):
                    for s in range(2):
                        n = 2 * g.at + s
                        if not g.last:
                            sp.wait_ge(xT_done, n + 1)
                            sp.dma_start(x[:, s, :], tile_of(x_tiles, n + 2)).then_inc(x_in[s], 16)
                        if not (g.first and s == 0):
                            sp.wait_ge(y_out, n)
                            sp.dma_start(tile_of(out_tiles, n - 1), y[:, 1 - s, :]).then_inc(stored[1 - s], 16)
                            if not (g.last and s):
                                sp.dma_start(x2[:, 1 - s, :], tile_of(x2_tiles, n + 1)).then_inc(x2_in[1 - s], 16)
                sp.wait_ge(y_out, NT)
                sp.dma_start(out_tiles[NT - 1], y[:, 1, :]).then_inc(stored[1], 16)
                for s in range(2):
                    sp.wait_ge(stored[s], 16 * (NT // 2))

            @block.gpsimd
            def _(pool):
                nc.gpsimd.memset(ident[:, :], 0.0).then_inc(pool_step, 1)
                nc.gpsimd.memset(before[:, :], 1.0).then_inc(pool_step, 1)
                nc.gpsimd.memset(ones[:, :], 1.0).then_inc(pool_setup, 1)
                nc.gpsimd.memset(carry[:, :, :], 1.0).then_inc(pool_step, 1)
                pool.wait_ge(pool_step, 3)
                nc.gpsimd.affine_select(out=ident[:, :], in_=ident[:, :], compare_op=ALU.not_equal, fill=1.0,
                                        base=0, pattern=[[-1, P]], channel_multiplier=1).then_inc(pool_setup, 1)
                nc.gpsimd.affine_select(out=before[:, :], in_=before[:, :], compare_op=ALU.is_gt, fill=0.0,
                                        base=0, pattern=[[1, P]], channel_multiplier=-1).then_inc(pool_setup, 1)
                nc.gpsimd.affine_select(out=carry[:, :, :], in_=carry[:, :, :], compare_op=ALU.not_equal, fill=0.0,
                                        base=0, pattern=[[0, E], [1, NT]], channel_multiplier=0).then_inc(pool_setup, 1)
                nc.gpsimd.iota(back[:, :, :], pattern=[[0, NT], [-1, E]], base=E, channel_multiplier=0,
                               allow_small_or_imprecise_dtypes=True).then_inc(pool_setup, 1)
                nc.gpsimd.iota(tiles_i[:, :, :], pattern=[[P, RT], [0, E]], base=0, channel_multiplier=0,
                               allow_small_or_imprecise_dtypes=True).then_inc(pool_setup, 1)
                nc.gpsimd.iota(entry[:, :, :, 0], pattern=[[0, TOP], [P, NT]], base=0, channel_multiplier=1,
                               allow_small_or_imprecise_dtypes=True).then_inc(pool_setup, 1)
                pool.wait_ge(slots_empty, 48)
                pool.wait_ge(routed, 1)
                for n in range(NT):
                    for k in range(TOP):
                        nc.gpsimd.indirect_dma_start(
                            out=table_dram[:, :], out_offset=bass.IndirectOffsetOnAxis(ap=slot_i[:, k, n:n + 1], axis=0),
                            in_=entry[:, k, n, :], in_offset=None).then_inc(sent, 16)
                pool.wait_ge(sent, 16 * TOP * NT)

            @block.scalar
            def _(act):
                nc.scalar.activation(gates[:, :, :], logits[:, :, :], ACT.Exp, scale=-1.0).then_inc(exp_done, 1)
                act.wait_ge(weights_in, 48)
                for raw, hi in ((w1_raw, w13_hi[:, 0]), (w3_raw, w13_hi[:, 1]), (w2_raw, w2_hi[:, :, :])):
                    nc.scalar.activation(hi, raw[:, :, :], ACT.Identity).then_inc(w_hi_done, 1)

                def x_upper(s, n):
                    act.wait_ge(xT_done, n)
                    nc.scalar.activation(xT_hi[:, s], pT[:, 0, 0:D].rearrange("p (c n) -> p c n", c=DC),
                                         ACT.Identity).then_inc(xT_hi_done, 1)

                def h_upper(n):
                    act.wait_ge(hT_done, n)
                    nc.scalar.activation(hT_hi[:, :, :], phT[:, 0, :].rearrange("p (c n) -> p c n", c=FC),
                                         ACT.Identity).then_inc(hT_hi_done, 1)

                x_upper(0, 1)
                for g in ahead(act):
                    for s in range(2):
                        n = 2 * g.at + s
                        if not (g.last and s):
                            x_upper(1 - s, n + 2)
                        if not (g.first and s == 0):
                            h_upper(n)
                        act.wait_ge(h1_done, n + 1)
                        nc.scalar.activation(act1[:, s, :], p1_[:, s, :], ACT.Silu).then_inc(silu_done, 1)
                h_upper(NT)

            @block.vector
            def _(dve):
                n_steps = [0]

                def link(ins):
                    n_steps[0] += 1
                    ins.then_inc(step, 1)
                    dve.wait_ge(step, n_steps[0])

                tt, ts = nc.vector.tensor_tensor, nc.vector.tensor_scalar

                def over_experts(a):
                    return a.unsqueeze(2).broadcast_to([P, NT, E])

                dve.wait_ge(exp_done, 1)
                link(ts(gates[:, :, :], gates[:, :, :], 1.0, None, ALU.add))
                link(nc.vector.reciprocal(gates[:, :, :], gates[:, :, :]))
                dve.wait_ge(pool_setup, 7)
                src = gates[:, :, :]
                for k in range(TOP):
                    link(nc.vector.tensor_reduce(top[:, k, :], src, AX_X, ALU.max))
                    link(tt(work[:, :, :], src, over_experts(top[:, k, :]), ALU.is_equal))
                    link(tt(work[:, :, :], work[:, :, :], back[:, :, :], ALU.mult))
                    link(nc.vector.tensor_reduce(norm[:, :], work[:, :, :], AX_X, ALU.max))
                    link(tt(hot[:, k], back[:, :, :], over_experts(norm[:, :]), ALU.is_equal))
                    if k == 0:
                        link(ts(work[:, :, :], hot[:, 0], -2.0, None, ALU.mult))
                        link(tt(rest[:, :, :], src, work[:, :, :], ALU.add))
                        src = rest[:, :, :]
                tt(both[:, :, :], hot[:, 0], hot[:, 1], ALU.add).then_inc(chosen, 1)
                dve.wait_ge(counted, 1)
                link(nc.vector.tensor_copy(totals[:, :, :], pr[:, 1, :].rearrange("p (n e) -> p e n", e=E)))
                link(nc.vector.tensor_tensor_scan(upto[:, :, :].rearrange("p e n -> p (e n)"),
                                                  carry[:, :, :].rearrange("p e n -> p (e n)"),
                                                  totals[:, :, :].rearrange("p e n -> p (e n)"), 0.0, ALU.mult, ALU.add))
                shift = P.bit_length() - 1
                link(ts(padded_i[:, :], upto[:, :, NT - 1], float(P - 1), None, ALU.add))
                link(ts(padded_i[:, :], padded_i[:, :], shift, shift, ALU.logical_shift_right, ALU.logical_shift_left))
                link(nc.vector.tensor_copy(padded[:, :], padded_i[:, :]))
                link(nc.vector.tensor_tensor_scan(ends[:, :], ones[:, 0:E], padded[:, :], 0.0, ALU.mult, ALU.add))
                link(tt(starts[:, :], ends[:, :], padded[:, :], ALU.subtract))
                link(tt(compare[:, :, :], tiles_i[:, :, :], ends[:, :].unsqueeze(1).broadcast_to([P, RT, E]), ALU.is_ge))
                link(nc.vector.tensor_reduce(owner[:, :], compare[:, :, :], AX_X, ALU.add))
                link(ts(expert_of[:, :], owner[:, :], float(E - 1), None, ALU.min))
                link(tt(upto[:, :, :], upto[:, :, :], totals[:, :, :], ALU.subtract))
                link(tt(upto[:, :, :], upto[:, :, :], starts[:, :].unsqueeze(2).broadcast_to([P, E, NT]), ALU.add))
                link(tt(work[:, :, :], pr[:, 0, :].rearrange("p (n e) -> p n e", e=E),
                        upto[:, :, :].rearrange("p e n -> p n e"), ALU.add))
                for k in range(TOP):
                    link(tt(rest[:, :, :], work[:, :, :], hot[:, k], ALU.mult))
                    link(nc.vector.tensor_reduce(slot[:, k, :], rest[:, :, :], AX_X, ALU.add))
                link(nc.vector.tensor_copy(slot_r[:, :, :], slot[:, :, :]))
                link(ts(slot_p[:, :, :], slot_r[:, :, :], P - 1, None, ALU.bitwise_and))
                link(nc.vector.tensor_copy(slot[:, :, :], slot_p[:, :, :]))
                link(ts(slot_r[:, :, :], slot_r[:, :, :], shift, None, ALU.logical_shift_right))
                link(nc.vector.tensor_copy(rank[:, :, :], slot_r[:, :, :]))
                link(nc.vector.scalar_tensor_tensor(out=slot[:, :, :], in0=slot[:, :, :], scalar=float(RT),
                                                    in1=rank[:, :, :], op0=ALU.mult, op1=ALU.add))
                link(nc.vector.tensor_copy(slot_i[:, :, :], slot[:, :, :]))
                link(tt(norm[:, :], top[:, 0, :], top[:, 1, :], ALU.add))
                link(nc.vector.reciprocal(norm[:, :], norm[:, :]))
                link(ts(norm[:, :], norm[:, :], OUT_SCALE, None, ALU.mult))
                tt(entry[:, :, :, 1], top[:, :, :], norm[:, :].unsqueeze(1).broadcast_to([P, TOP, NT]), ALU.mult
                   ).then_inc(routed, 1)

                dve.wait_ge(weights_in, 48)
                dve.wait_ge(w_hi_done, 3)
                for raw, hi, lo in ((w1_raw, w13_hi[:, 0], w13_lo[:, 0]), (w3_raw, w13_hi[:, 1], w13_lo[:, 1]),
                                    (w2_raw, w2_hi[:, :, :], w2_lo[:, :, :])):
                    tt(lo, raw[:, :, :], hi, ALU.subtract).then_inc(w_lo_done, 1)

                def x_lower(s, n):
                    dve.wait_ge(xT_hi_done, n)
                    tt(xT_lo[:, s], pT[:, 0, 0:D].rearrange("p (c n) -> p c n", c=DC), xT_hi[:, s],
                       ALU.subtract).then_inc(xT_lo_done, 1)

                def h_lower(n):
                    dve.wait_ge(hT_hi_done, n)
                    tt(hT_lo[:, :, :], phT[:, 0, :].rearrange("p (c n) -> p c n", c=FC), hT_hi[:, :, :],
                       ALU.subtract).then_inc(hT_lo_done, 1)

                def add_y(g, s, n):
                    o = 1 - s
                    dve.wait_ge(y_done, n)
                    dve.wait_ge(x2_in[o], 16 * (g + s))
                    if not isinstance(g, int) or g + s > 1:
                        dve.wait_ge(stored[o], 16 * (g + s - 1))
                    nc.vector.scalar_tensor_tensor(out=y[:, o, :], in0=py[:, 0, 0:D], scalar=OUT_SCALE, in1=x2[:, o, :],
                                                   op0=ALU.mult, op1=ALU.add).then_inc(y_out, 1)

                x_lower(0, 1)
                for g in ahead(dve):
                    for s in range(2):
                        n = 2 * g.at + s
                        if not (g.last and s):
                            x_lower(1 - s, n + 2)
                        if not (g.first and s == 0):
                            h_lower(n)
                        dve.wait_ge(silu_done, n + 1)
                        dve.wait_ge(h3_done, n + 1)
                        tt(h[:, s, :], p3_[:, s, :], act1[:, s, :], ALU.mult).then_inc(h_done, 1)
                        if not (g.first and s == 0):
                            add_y(g.at, s, n)
                h_lower(NT)
                add_y(NT // 2, 0, NT)

            @block.tensor
            def _(pe):
                def exact3(out, pairs, start=True, stop=True):
                    n = 0
                    for (lh, ll), (rh, rl) in pairs:
                        for a, b in ((lh, rh), (lh, rl), (ll, rh)):
                            last = nc.tensor.matmul(out, a, b, start=(n == 0), stop=(n == 3 * len(pairs) - 1))
                            n += 1
                    return last

                pe.wait_ge(pool_setup, 7)
                pe.wait_ge(chosen, 1)
                chosen_v = both[:, :, :].rearrange("p n e -> p (n e)")
                nc.tensor.matmul(pr[:, 0, :], before[:, :], chosen_v, start=True, stop=True)
                nc.tensor.matmul(pr[:, 1, :], ones[:, :], chosen_v, start=True, stop=True).then_inc(counted, 1)

                def transpose_x(s, n, loads):
                    pe.wait_ge(x_in[s], 16 * loads)
                    if not (isinstance(n, int) and n == 1):
                        pe.wait_ge(xT_lo_done, n - 1)
                    for c in range(DC):
                        last = nc.tensor.transpose(pT[:, 0, c * P:(c + 1) * P], x[:, s, c * P:(c + 1) * P], ident[:, :])
                    last.then_inc(xT_done, 1)

                def transpose_h(s, n):
                    pe.wait_ge(h_done, n)
                    for c in range(FC):
                        last = nc.tensor.transpose(phT[:, 0, c * P:(c + 1) * P], h[:, s, c * P:(c + 1) * P], ident[:, :])
                    last.then_inc(hT_done, 1)

                def down(n):
                    pe.wait_ge(hT_lo_done, n)
                    if not (isinstance(n, int) and n == 1):
                        pe.wait_ge(y_out, n - 1)
                    exact3(py[:, 0, 0:D], [((hT_hi[:, c, :], hT_lo[:, c, :]), (w2_hi[:, c, :], w2_lo[:, c, :]))
                                           for c in range(FC)]).then_inc(y_done, 1)

                transpose_x(0, 1, 1)
                pe.wait_ge(w_lo_done, 3)
                for g in ahead(pe):
                    for s in range(2):
                        n = 2 * g.at + s
                        if not (g.last and s):
                            transpose_x(1 - s, n + 2, g.at + 1 + s)
                        if not (g.first and s == 0):
                            transpose_h(1 - s, n)
                        pe.wait_ge(xT_lo_done, n + 1)
                        for j, (bank, done) in enumerate(((p1_, h1_done), (p3_, h3_done))):
                            if not (g.first):
                                pe.wait_ge((silu_done, h_done)[j], n - 1)
                            exact3(bank[:, s, :], [((xT_hi[:, s, c, :], xT_lo[:, s, c, :]),
                                                    (w13_hi[:, j, c, :], w13_lo[:, j, c, :])) for c in range(DC)]
                                   ).then_inc(done, 1)
                        if not (g.first and s == 0):
                            down(n)
                transpose_h(1, NT)
                down(NT)


def routed_experts(nc, xl_dram, table_dram, out, experts, experts_in, expert_of):
    w1, w3, w2 = experts
    with ExitStack() as ctx:
        def sb(name, shape, dt=F32):
            return ctx.enter_context(nc.sbuf_tensor("r_" + name, shape, dt))

        def sem(name):
            return ctx.enter_context(nc.semaphore("r_" + name))

        ident = sb("ident", [P, P])
        w1_hi = sb("w1_hi", [P, E, DC, F], F32R)
        w3_hi = sb("w3_hi", [P, E, DC, F], F32R)
        table = sb("table", [P, RT, 2])
        tokens = sb("tokens", [P, RT], U32)
        index = sb("index", [P, U], U32)
        x = sb("x", [P, U, D])
        xT_hi = sb("xT_hi", [P, 2, DC, P], F32R)
        xT_lo = sb("xT_lo", [P, 2, DC, P], F32R)
        act1 = sb("act1", [P, 2, F])
        h = sb("h", [P, 2, F])
        hT = sb("hT", [P, 2, FC, P])
        y = sb("y", [P, YB, D])

        def ps(name, n):
            return ctx.enter_context(nc.psum_tensor("r_" + name, [P, n, 512], F32))

        pT, p1_, p3_, phT, py = ps("pT", 1), ps("p1", 2), ps("p3", 2), ps("phT", 1), ps("py", 2)

        pool_setup = sem("pool_setup")
        pool_step = sem("pool_step")
        table_in = sem("table_in")
        tokens_done = sem("tokens_done")
        index_done = sem("index_done")
        w_hi_done = sem("w_hi_done")
        w_lo_done = sem("w_lo_done")
        x_in = sem("x_in")
        xT_done = sem("xT_done")
        xT_hi_done = sem("xT_hi_done")
        xT_lo_done = sem("xT_lo_done")
        h1_done = sem("h1_done")
        h3_done = sem("h3_done")
        silu_done = sem("silu_done")
        h_done = sem("h_done")
        hT_done = sem("hT_done")
        hT_out = sem("hT_out")
        y_done = sem("y_done")
        y_out = sem("y_out")
        pool_past = sem("pool_past")
        added = sem("added")

        def several(eng):
            yield Turn(0, first=True)
            with eng.Fori(1, RT // U - 1) as g:
                yield Turn(g)
            yield Turn(RT // U - 1, last=True)

        def at(n):
            return slice(n, n + 1) if isinstance(n, int) else bass.ds(n, 1)

        with nc.Block() as block:
            @block.sync
            def _(sp):
                sp.dma_start(table[:, :, :], table_dram.rearrange("(p j) c -> p j c", p=P)).then_inc(table_in, 16)

            @block.gpsimd
            def _(pool):
                def gather(s, n):
                    nc.gpsimd.tensor_copy(index[:, s:s + 1], tokens[:, at(n)]).then_inc(index_done, 1)
                    pool.wait_ge(index_done, n + 1)
                    pool.sem_inc(pool_past, 1)
                    nc.gpsimd.indirect_dma_start(
                        out=x[:, s, :], out_offset=None, in_=xl_dram[:, :],
                        in_offset=bass.IndirectOffsetOnAxis(ap=index[:, s:s + 1], axis=0)).then_inc(x_in, 16)

                nc.gpsimd.memset(ident[:, :], 0.0).then_inc(pool_step, 1)
                pool.wait_ge(pool_step, 1)
                nc.gpsimd.affine_select(out=ident[:, :], in_=ident[:, :], compare_op=ALU.not_equal, fill=1.0,
                                        base=0, pattern=[[-1, P]], channel_multiplier=1).then_inc(pool_setup, 1)
                pool.wait_ge(tokens_done, 1)
                for n in range(GATHERED):
                    if n:
                        pool.wait_ge(x_in, 16 * n)
                    gather(n, n)
                for g in several(pool):
                    for s in range(U):
                        n = U * g.at + s
                        if not (g.last and s + GATHERED >= U):
                            pool.wait_ge(x_in, 16 * (n + GATHERED))
                            if not (g.first and s + GATHERED < U):
                                pool.wait_ge(xT_done, n + GATHERED - U + 1)
                            gather((s + GATHERED) % U, n + GATHERED)
                        pool.wait_ge(y_out, n + 1)
                        if not (g.first and s == 0):
                            pool.wait_ge(added, 16 * n)
                        pool.sem_inc(pool_past, 1)
                        nc.gpsimd.indirect_dma_start(
                            out=out[:, :], out_offset=bass.IndirectOffsetOnAxis(ap=index[:, s:s + 1], axis=0),
                            in_=y[:, s % YB, :], in_offset=None, compute_op=ALU.add).then_inc(added, 16)
                pool.wait_ge(added, 16 * RT)

            @block.scalar
            def _(act):
                def x_upper(s, n):
                    act.wait_ge(xT_done, n)
                    nc.scalar.activation(xT_hi[:, s], pT[:, 0, 0:D].rearrange("p (c n) -> p c n", c=DC),
                                         ACT.Identity).then_inc(xT_hi_done, 1)

                def h_out(s, n):
                    act.wait_ge(hT_done, n)
                    nc.scalar.activation(hT[:, s], phT[:, 0, :].rearrange("p (c n) -> p c n", c=FC),
                                         ACT.Identity).then_inc(hT_out, 1)

                act.wait_ge(experts_in, 16 * 3 * E)
                for e in range(E):
                    for w, hi in ((w1, w1_hi), (w3, w3_hi)):
                        nc.scalar.activation(hi[:, e], w[:, e].bitcast(F32), ACT.Identity).then_inc(w_hi_done, 1)
                x_upper(0, 1)
                for g in several(act):
                    for s in range(U):
                        n = U * g.at + s
                        if not (g.last and s == U - 1):
                            x_upper((s + 1) % 2, n + 2)
                        if not (g.first and s == 0):
                            h_out((s + 1) % 2, n)
                        act.wait_ge(h1_done, n + 1)
                        nc.scalar.activation(act1[:, s % 2, :], p1_[:, s % 2, :], ACT.Silu).then_inc(silu_done, 1)
                h_out(1, RT)

            @block.vector
            def _(dve):
                def x_lower(s, n):
                    dve.wait_ge(xT_hi_done, n)
                    nc.vector.tensor_tensor(xT_lo[:, s], pT[:, 0, 0:D].rearrange("p (c n) -> p c n", c=DC), xT_hi[:, s],
                                            ALU.subtract).then_inc(xT_lo_done, 1)

                def weigh(g, s, n):
                    o = (s - 1) % YB
                    dve.wait_ge(y_done, n)
                    if not isinstance(n, int) or n > YB:
                        dve.wait_ge(added, 16 * (n - YB))
                    nc.vector.tensor_scalar(y[:, o, :], py[:, o % 2, 0:D], table[:, at(n - 1), 1], None,
                                            ALU.mult).then_inc(y_out, 1)

                dve.wait_ge(table_in, 16)
                nc.vector.tensor_copy(tokens[:, :], table[:, :, 0]).then_inc(tokens_done, 1)
                for e in range(E):
                    for i, (w, hi) in enumerate(((w1, w1_hi), (w3, w3_hi))):
                        dve.wait_ge(w_hi_done, 2 * e + i + 1)
                        nc.vector.tensor_tensor(w[:, e], w[:, e].bitcast(F32), hi[:, e], ALU.subtract).then_inc(w_lo_done, 1)
                x_lower(0, 1)
                for g in several(dve):
                    for s in range(U):
                        n = U * g.at + s
                        if not (g.last and s == U - 1):
                            x_lower((s + 1) % 2, n + 2)
                        dve.wait_ge(silu_done, n + 1)
                        dve.wait_ge(h3_done, n + 1)
                        nc.vector.tensor_tensor(h[:, s % 2, :], p3_[:, s % 2, :], act1[:, s % 2, :], ALU.mult).then_inc(h_done, 1)
                        if not (g.first and s == 0):
                            weigh(g, s, n)
                weigh(None, 0, RT)

            @block.tensor
            def _(pe):
                def expert(n):
                    return pe.value_load(expert_of[0:1, at(n)], min_val=0, max_val=E - 1)

                def of(w, e, c):
                    return w[:, bass.ds(e, 1), c, :].rearrange("p a n -> p (a n)")

                def transpose_x(s, n):
                    pe.wait_ge(x_in, 16 * n)
                    if not (isinstance(n, int) and n == 1):
                        pe.wait_ge(xT_lo_done, n - 1)
                    for c in range(DC):
                        last = nc.tensor.transpose(pT[:, 0, c * P:(c + 1) * P], x[:, s, c * P:(c + 1) * P], ident[:, :])
                    last.then_inc(xT_done, 1)

                def transpose_h(s, n):
                    pe.wait_ge(h_done, n)
                    if not (isinstance(n, int) and n == 1):
                        pe.wait_ge(hT_out, n - 1)
                    for c in range(FC):
                        last = nc.tensor.transpose(phT[:, 0, c * P:(c + 1) * P], h[:, s, c * P:(c + 1) * P], ident[:, :])
                    last.then_inc(hT_done, 1)

                def down(s, n):
                    e = expert(n - 1)
                    pe.wait_ge(hT_out, n)
                    if not (isinstance(n, int) and n < 3):
                        pe.wait_ge(y_out, n - 2)
                    for c in range(FC):
                        last = nc.tensor.matmul(py[:, s, 0:D], hT[:, s, c, :], of(w2, e, c),
                                                start=(c == 0), stop=(c == FC - 1))
                    last.then_inc(y_done, 1)

                pe.wait_ge(pool_setup, 1)
                transpose_x(0, 1)
                pe.wait_ge(w_lo_done, 2 * E)
                for g in several(pe):
                    for s in range(U):
                        n = U * g.at + s
                        e = expert(n)
                        if not (g.last and s == U - 1):
                            transpose_x((s + 1) % U, n + 2)
                        if not (g.first and s == 0):
                            transpose_h((s + 1) % 2, n)
                        pe.wait_ge(xT_lo_done, n + 1)
                        for j, (bank, done, hi, lo) in enumerate(((p1_, h1_done, w1_hi, w1), (p3_, h3_done, w3_hi, w3))):
                            if not (g.first and s < 2):
                                pe.wait_ge((silu_done, h_done)[j], n - 1)
                            for c in range(DC):
                                for i, (a, w) in enumerate(((xT_hi, hi), (xT_hi, lo), (xT_lo, hi))):
                                    last = nc.tensor.matmul(bank[:, s % 2, :], a[:, s % 2, c, :], of(w, e, c),
                                                            start=(c == 0 and i == 0), stop=(c == DC - 1 and i == 2))
                            last.then_inc(done, 1)
                        if not (g.first and s == 0):
                            down((s + 1) % 2, n)
                transpose_h(1, RT)
                down(1, RT)


def transformer_block(nc, t, out):
    x1 = nc.dram_tensor("x1_stream", (TOKENS, D), F32, kind="Internal").ap()
    x2 = nc.dram_tensor("x2_stream", (TOKENS, D), F32, kind="Internal").ap()
    xl = nc.dram_tensor("x2_normalised", (OUT_ROWS, D), F32, kind="Internal").ap()
    table = nc.dram_tensor("slot_table", (SLOTS, 2), F32, kind="Internal").ap()
    cross_attention(nc, t, x1)
    with ExitStack() as ctx:
        logits = ctx.enter_context(nc.sbuf_tensor("logits", [P, NT, E], F32))
        empty = ctx.enter_context(nc.sbuf_tensor("empty", [P, RT, 2], F32))
        zeros = ctx.enter_context(nc.sbuf_tensor("zeros", [P, D], F32))
        expert_of = ctx.enter_context(nc.sbuf_tensor("expert_of", [P, RT], I32))
        w1 = ctx.enter_context(nc.sbuf_tensor("experts_w1", [P, E, DC, F], F32R))
        w3 = ctx.enter_context(nc.sbuf_tensor("experts_w3", [P, E, DC, F], F32R))
        w2 = ctx.enter_context(nc.sbuf_tensor("experts_w2", [P, E, FC, D], F32))
        empty_set = ctx.enter_context(nc.semaphore("empty_set"))
        slots_empty = ctx.enter_context(nc.semaphore("slots_empty"))
        experts_in = ctx.enter_context(nc.semaphore("experts_in"))
        with nc.Block() as block:
            @block.gpsimd
            def _(pool):
                nc.gpsimd.memset(empty[:, :, :], 0.0).then_inc(empty_set, 1)
                nc.gpsimd.memset(zeros[:, :], 0.0).then_inc(empty_set, 1)
                pool.wait_ge(empty_set, 2)
                nc.gpsimd.iota(empty[:, :, 0], pattern=[[0, RT]], base=TOKENS, channel_multiplier=1,
                               allow_small_or_imprecise_dtypes=True).then_inc(empty_set, 1)

        def load_ahead(eng):
            eng.wait_ge(empty_set, 3)
            empty_slots(eng, table, xl, out, empty, zeros, slots_empty)
            load_experts(eng, t, (w1, w3, w2), experts_in)

        self_attention(nc, t, x1, x2, xl, logits, load_ahead)
        shared_expert(nc, t, x2, xl, table, out, logits, slots_empty, expert_of)
        routed_experts(nc, xl, table, out, (w1, w3, w2), experts_in, expert_of)


_INS = ["x", "ctx_1024"] + [f"L0_xattn_{n}" for n in ("Wq", "bq", "Wk", "bk", "Wv", "bv", "Wo", "bo", "ln_gamma", "ln_beta")] \
    + [f"L0_attn_{n}" for n in ("Wq", "bq", "Wk", "bk", "Wv", "bv", "Wo", "bo")] \
    + [f"L0_ffn_{n}" for n in ("Wg", "Ws1", "Ws3", "Ws2", "We1", "We3", "We2")]


def kernel(**inputs):
    import concourse.bacc as _bacc
    from concourse.bass_utils import run_bass_kernel_spmd as _run

    nc = _bacc.Bacc("TRN2", target_bir_lowering=False, num_devices=1)
    arrays, tensors = {}, {}
    for name in _INS + ["rope"]:
        a = rope_tables() if name == "rope" else np.ascontiguousarray(inputs[name])
        arrays[f"in_{name}_dram"] = a
        tensors[name] = nc.dram_tensor(f"in_{name}_dram", a.shape, mybir.dt.from_np(a.dtype), kind="ExternalInput").ap()
    out = nc.dram_tensor("out_0_dram", (OUT_ROWS, D), F32, kind="ExternalOutput").ap()
    transformer_block(nc, tensors, out)
    r = _run(nc, [arrays], core_ids=[0])
    return np.asarray(r.results[0]["out_0_dram"])[:TOKENS].reshape(BATCH, SQ, D)
```
